# Optimizing a Trainium2 kernel written in Bass

```python
import numpy as np
import jax
import jax.numpy as jnp

def _softmax(x, axis=-1):
    return jax.nn.softmax(x, axis=axis)

def _gelu(x):
    return jax.nn.gelu(x, approximate=True)

def _silu(x):
    return jax.nn.silu(x)

def _sigmoid(x):
    return jax.nn.sigmoid(x)

def _layernorm(x, axis=-1, eps=1e-05):
    m = jnp.mean(x, axis=axis, keepdims=True)
    v = jnp.var(x, axis=axis, keepdims=True)
    return (x - m) / jnp.sqrt(v + eps)

def _scatter_add(tgt, idx, src, axis=0):
    return tgt.at[idx].add(src)

def _segment_sum(src, seg, n):
    return jax.ops.segment_sum(src, seg, n)
kernel_name = 'mk_adj_resnorm_d2_adj_r2_1b96e1'

def setup_inputs(seed: int=0):
    np.random.seed(seed)
    _w = jnp.asarray

    def _rec_inputs():
        import jax
        import jax.numpy as jnp
        _gk = jax.random.key(seed)
        x = -0.0005207 + 1.001 * jax.random.normal(jax.random.fold_in(_gk, 1), (16, 512, 256), jnp.float32)
        _w = (1.0 + jnp.arange(512, dtype=jnp.float32)) ** (-0.5)
        _w = _w / _w.mean()
        _pij = jnp.clip(0.00390625 * _w[:, None] * _w[None, :], 0.0, 1.0)
        _a = jax.random.uniform(jax.random.fold_in(_gk, 2), (16, 512, 512)) < _pij
        _af = _a.astype(jnp.float32)
        adj = _af
        _nm = jnp.ones((16, 512), dtype=bool)
        nodemask = _nm
        return (x, adj, nodemask)
    x, adj, nodemask = _rec_inputs()

    def _L0_gnn_setup():
        import jax, jax.numpy as jnp
        import numpy as np
        HEADS = 8
        DIM_HEAD = 64
        LA = 0.33
        LD = 0.33
        LG = 0.33
        key = jax.random.key(seed)
        ks = jax.random.split(key, 6)
        B, N, D = (4, 512, 256)
        inner = HEADS * DIM_HEAD
        x = jax.random.normal(ks[0], (B, N, D), jnp.float32)
        mask = jax.random.uniform(ks[1], (B, N)) < 0.9
        adjacency_mat = (jax.random.uniform(ks[2], (B, N, N)) < 0.05).astype(jnp.float32)
        distance_mat = jax.random.uniform(ks[3], (B, N, N), jnp.float32) * 5.0
        W_qkv = jax.random.normal(ks[4], (D, inner * 3), jnp.float32) * 0.02
        W_out = jax.random.normal(ks[5], (inner, D), jnp.float32) * 0.02
        b_out = jnp.zeros((D,), jnp.float32)
        return {'x': x, 'mask': mask, 'adjacency_mat': adjacency_mat, 'distance_mat': distance_mat, 'W_qkv': W_qkv, 'W_out': W_out, 'b_out': b_out}
    _L0_gnn_all = _L0_gnn_setup()
    _L0_gnn_in = {k: v for k, v in _L0_gnn_all.items() if k in ('W_qkv', 'W_out', 'b_out')}
    del _L0_gnn_all

    def _L1_gnn_setup():
        import jax, jax.numpy as jnp
        import numpy as np
        B, N, DIN, DOUT, K = (4, 1024, 256, 256, 3)
        key = jax.random.key(seed)
        ks = jax.random.split(key, 8)
        X = jax.random.normal(ks[0], (B, N, DIN), dtype=jnp.float32)
        A = jax.random.uniform(ks[1], (B, N, N), dtype=jnp.float32)
        Wv = jax.random.normal(ks[2], (DIN, DOUT), dtype=jnp.float32) * 0.02
        bv = jax.random.normal(ks[3], (DOUT,), dtype=jnp.float32) * 0.02
        aw = jax.random.normal(ks[4], (2 * DOUT, 1), dtype=jnp.float32) * 0.05
        ab = jax.random.normal(ks[5], (1,), dtype=jnp.float32) * 0.05
        Wk = jax.random.normal(ks[6], (K, DIN, DOUT), dtype=jnp.float32) * 0.02
        bk = jax.random.normal(ks[7], (K, DOUT), dtype=jnp.float32) * 0.02
        return {'X': X, 'A': A, 'Wv': Wv, 'bv': bv, 'aw': aw, 'ab': ab, 'Wk': Wk, 'bk': bk}
    _L1_gnn_all = _L1_gnn_setup()
    _L1_gnn_in = {k: v for k, v in _L1_gnn_all.items() if k in ('Wv', 'bv', 'aw', 'ab', 'Wk', 'bk')}
    del _L1_gnn_all
    return {'x': x, 'adj': adj, 'nodemask': nodemask, 'L0_gnn_W_qkv': _L0_gnn_in['W_qkv'], 'L0_gnn_W_out': _L0_gnn_in['W_out'], 'L0_gnn_b_out': _L0_gnn_in['b_out'], 'L1_gnn_Wv': _L1_gnn_in['Wv'], 'L1_gnn_bv': _L1_gnn_in['bv'], 'L1_gnn_aw': _L1_gnn_in['aw'], 'L1_gnn_ab': _L1_gnn_in['ab'], 'L1_gnn_Wk': _L1_gnn_in['Wk'], 'L1_gnn_bk': _L1_gnn_in['bk']}

def reference(x, adj, nodemask, L0_gnn_W_qkv, L0_gnn_W_out, L0_gnn_b_out, L1_gnn_Wv, L1_gnn_bv, L1_gnn_aw, L1_gnn_ab, L1_gnn_Wk, L1_gnn_bk):
    import jax
    import jax.numpy as jnp

    def _L0_gnn_ref(x, mask, adjacency_mat, distance_mat, W_qkv, W_out, b_out):
        import jax, jax.numpy as jnp
        import numpy as np
        HEADS = 8
        DIM_HEAD = 64
        LA = 0.33
        LD = 0.33
        LG = 0.33
        B, N, _ = x.shape
        scale = DIM_HEAD ** (-0.5)
        qkv = (x @ W_qkv).reshape(B, N, HEADS, 3, DIM_HEAD)
        q, k, v = (jnp.transpose(qkv[..., i, :], (0, 2, 1, 3)) for i in range(3))
        dots = jnp.einsum('bhid,bhjd->bhij', q, k) * scale
        big = jnp.finfo(dots.dtype).max
        m2 = mask[:, None, :, None] & mask[:, None, None, :]
        dots = jnp.where(m2, dots, -big)
        attn = jax.nn.softmax(dots, axis=-1) * LA
        adj = jnp.where(m2, adjacency_mat[:, None], 0.0)
        dist = jnp.where(m2, distance_mat[:, None], big)
        attn = attn + LG * adj + LD * jnp.exp(-dist)
        out = jnp.einsum('bhij,bhjd->bhid', attn, v)
        out = jnp.transpose(out, (0, 2, 1, 3)).reshape(B, N, HEADS * DIM_HEAD)
        return out @ W_out + b_out

    def _L1_gnn_ref(X, A, Wv, bv, aw, ab, Wk, bk):
        import jax, jax.numpy as jnp
        import numpy as np
        B, N, DIN, DOUT, K = (4, 1024, 256, 256, 3)
        d = Wv.shape[1]
        Xw = X @ Wv + bv
        sj = Xw @ aw[:d, 0]
        si = Xw @ aw[d:, 0]
        e = jax.nn.leaky_relu(sj[:, None, :] + si[:, :, None] + ab[0], negative_slope=0.2)
        alpha_matrix = A * jnp.exp(e)
        transition = alpha_matrix / (jnp.sum(alpha_matrix, axis=-1, keepdims=True) + 1e-12)
        H = jnp.zeros(X.shape[:-1] + (d,), dtype=X.dtype)
        Xk = X
        for k in range(Wk.shape[0]):
            H = H + Xk @ Wk[k] + bk[k]
            Xk = jnp.einsum('bij,bjd->bid', transition, Xk)
        return jax.nn.relu(H)
    x = _layernorm(x + _L0_gnn_ref(x, nodemask, adj, adj, L0_gnn_W_qkv, L0_gnn_W_out, L0_gnn_b_out), axis=-1)
    x = _layernorm(x + _L1_gnn_ref(x, adj, L1_gnn_Wv, L1_gnn_bv, L1_gnn_aw, L1_gnn_ab, L1_gnn_Wk, L1_gnn_bk), axis=-1)
    return x

_drawn_inputs = setup_inputs


def setup_inputs(seed=0):
    import zlib

    import numpy as np

    out = dict(_drawn_inputs(seed))
    spreads = {'L0_gnn_b_out': (0.0, 0.1)}
    factors = {'L1_gnn_Wv': 7.169, 'L1_gnn_bv': 8.0, 'L1_gnn_aw': 7.447}
    for name, (base, spread) in spreads.items():
        noise = np.random.default_rng([zlib.crc32(name.encode()), seed]).standard_normal(out[name].shape)
        drawn = base * np.exp(spread * noise) if base else spread * noise
        out[name] = jnp.asarray(drawn.astype(out[name].dtype))
    for name, factor in factors.items():
        out[name] = (out[name] * factor).astype(out[name].dtype)
    return out
```

```python
from contextlib import ExitStack

import concourse.bass as bass
from concourse import mybir

P = 128
F32 = mybir.dt.float32
F32R = mybir.dt.float32r
U8 = mybir.dt.uint8
ALU = mybir.AluOpType
ACT = mybir.ActivationFunctionType

HEADS = 8
DH = 64
GAIN = 0.33
SCORE_SCALE = DH ** -0.5
SLOPE = 0.2
EPS_NORM = 1e-5
EPS_SUM = 1e-12
MASKED = 1e30
LOWEST = -3.0e38

LAYER0_JOBS = (
    [(-1, "x_transpose", 0), (-1, "x_transpose", 1), (-1, "query", 0), (-1, "key", 0),
     (-1, "value", 0), (-1, "value", 1), (0, "value", 2), (1, "value", 3),
     (4, "query", 1), (5, "key", 1), (12, "query", 2), (13, "key", 2), (20, "query", 3), (21, "key", 3),
     (23, "mixed_value", 0), (25, "mixed_value", 1)]
    + [(27 + j, "adj_transpose", j) for j in range(4)]
    + [(32, "adj_product", 0), (34, "adj_product", 1)]
    + [(34, "head_transpose", 0), (34, "head_transpose", 1), (34, "out_product", 0),
       (34, "head_transpose", 2), (34, "head_transpose", 3), (34, "out_product", 1)])
LAYER1_JOBS = (
    [(2, "x1_transpose", 0), (3, "x1_transpose", 1), (6, "hop0", 0), (7, "hop0", 1), (8, "hop0", 2),
     (9, "hop0", 3), (10, "source_score", 0), (11, "hop12", 0), (14, "hop12", 1), (15, "hop12", 2),
     (16, "hop12", 3)]
    + [(s, "diffuse2", j) for j, s in enumerate((17, 18, 19, 22))]
    + [(24, "diffuse1", 0), (26, "diffuse1", 1)])
SPLIT_JOBS = ("x_transpose", "query", "key", "x1_transpose")
RING = 3


class Plan:

    def __init__(self, layer0, layer1, offset):
        jobs = (LAYER0_JOBS if layer0 else []) + (LAYER1_JOBS if layer1 else [])
        self.jobs = sorted(jobs, key=lambda j: j[0])
        self.layer0, self.layer1 = layer0, layer1
        self.slots = {}
        self.order, self.bank, self.split = {}, {}, {}
        for n, (slot, name, index) in enumerate(self.jobs):
            bank = (n + offset) % RING
            self.slots.setdefault(slot, []).append((name, index))
            self.order[name, index] = n
            self.bank[name, index] = bank
            if name in SPLIT_JOBS:
                self.split[name, index] = len(self.split)


FULL = Plan(True, True, 0)
FIRST = Plan(True, False, (-len(LAYER0_JOBS)) % RING)
LAST = Plan(False, True, 0)
assert len(FULL.jobs) % RING == 0


class Signal:

    def __init__(self, sem, first, full):
        self.sem, self.first, self.full = sem, first, full

    def total(self, step, count, unit=1):
        if isinstance(step, int):
            return ((0 if step == 0 else self.first + (step - 1) * self.full) + count) * unit
        assert self.first + count > 0, "a wait on a register must be on a value above zero"
        return step * (self.full * unit) + (self.first - self.full + count) * unit

    def wait(self, eng, step, count, unit=1):
        value = self.total(step, count, unit)
        if not isinstance(value, int) or value > 0:
            eng.wait_ge(self.sem, value)


def graph_layers(nc, x, adj, nodemask, w_qkv, w_out, b_out, w_v, b_v, att_w, att_b, w_k, b_k, out):
    B, N, D = x.shape
    NT = N // P
    KT = D // P
    HD = HEADS * DH
    HT = HD // P
    PAIRS = HEADS // 2
    UNITS = HEADS * NT
    HOPS = w_k.shape[0]
    assert NT == 4 and KT == 2 and HT == 4 and HOPS == 3 and N == 512

    ctx = ExitStack()
    with ctx:
        def sb(name, shape, dt=F32):
            return ctx.enter_context(nc.sbuf_tensor(name, shape, dt))

        def sem(name):
            return ctx.enter_context(nc.semaphore(name))

        def every(name, count):
            return Signal(sem(name), count, count)

        def layer1_only(name, count):
            return Signal(sem(name), 0, count)

        x_in = sb("x_in", [P, NT, D])
        adj_in = sb("adj_in", [P, NT, N])
        mask_in = sb("mask_in", [P, N], U8)
        x_bias = sb("x_bias", [P, NT, D])
        x_hi, x_lo = sb("x_hi", [P, KT, N], F32R), sb("x_lo", [P, KT, N], F32R)
        q_hi, q_lo = sb("q_hi", [P, 2, N], F32R), sb("q_lo", [P, 2, N], F32R)
        k_hi, k_lo = sb("k_hi", [P, 2, N], F32R), sb("k_lo", [P, 2, N], F32R)
        value = sb("value", [P, NT, HD])
        mixed = sb("mixed", [P, NT, D])
        column_bias = sb("column_bias", [P, N])
        row_mask = sb("row_mask", [P, NT])
        row_scale = sb("row_scale", [P, NT])
        row_neg_scale = sb("row_neg_scale", [P, NT])
        scores = sb("scores", [P, 2, N])
        row_max = sb("row_max", [P, 2])
        exp_bias = sb("exp_bias", [P, 2])
        row_sum = sb("row_sum", [P, 2, NT])
        row_inv = sb("row_inv", [P, 2, NT])
        probs = sb("probs", [P, 2, N])
        probs_t = sb("probs_t", [P, 2, N])
        heads_out = sb("heads_out", [P, NT, HD])
        heads_t = sb("heads_t", [P, 2, HD])
        adj_t = sb("adj_t", [P, NT, N])
        edge = sb("edge", [P, NT, N])
        exps = sb("exps", [P, 2, N])
        mix = sb("mix", [P, NT, D])
        x1 = sb("x1", [P, NT, D])
        x1_hi, x1_lo = sb("x1_hi", [P, KT, N], F32R), sb("x1_lo", [P, KT, N], F32R)
        hop0 = sb("hop0", [P, NT, D])
        hop1 = sb("hop1", [P, NT, D])
        hop1_full = sb("hop1_full", [P, NT, D])
        hop2 = sb("hop2", [P, NT, D + 2])
        target_score = sb("target_score", [P, NT])
        leaky = sb("leaky", [P, 2, N])
        alpha = sb("alpha", [P, NT, N])
        alpha_inv = sb("alpha_inv", [P, NT])
        alpha_sum = sb("alpha_sum", [P, NT])
        y = sb("y", [P, NT, D])
        stats0, stats1 = sb("stats0", [P, NT, 6]), sb("stats1", [P, NT, 6])
        mean0, mean1 = sb("mean0", [P, NT, 2]), sb("mean1", [P, NT, 2])
        var0, var1 = sb("var0", [P, NT]), sb("var1", [P, NT])
        rstd0, rstd1 = sb("rstd0", [P, NT]), sb("rstd1", [P, NT])

        wait_carrier = sb("wait_carrier", [P, 1])

        ident = sb("ident", [P, P])
        ones = sb("ones", [P, P])
        neg_half = sb("neg_half", [P, NT])
        mask_col = sb("mask_col", [P, B * NT])
        wqkv_hi = sb("wqkv_hi", [P, KT, 3, HD], F32R)
        wqkv_lo = sb("wqkv_lo", [P, KT, 3, HD], F32R)
        wout = sb("wout", [P, HT, D])
        wmix_hi, wmix_lo = sb("wmix_hi", [P, KT, D], F32R), sb("wmix_lo", [P, KT, D], F32R)
        w12_hi, w12_lo = sb("w12_hi", [P, KT, 2 * D], F32R), sb("w12_lo", [P, KT, 2 * D], F32R)
        w0_hi, w0_lo = sb("w0_hi", [P, KT, D + 2], F32R), sb("w0_lo", [P, KT, D + 2], F32R)
        wsrc_hi, wsrc_lo = sb("wsrc_hi", [P, KT, P], F32R), sb("wsrc_lo", [P, KT, P], F32R)
        b_out_all = sb("b_out_all", [P, D])
        bk_sum = sb("bk_sum", [P, D])
        score_const = sb("score_const", [P, 1])

        wqkv_raw = [edge[:, :, :].rearrange("p a b -> p (a b)")[:, 0:3 * HD],
                    alpha[:, :, :].rearrange("p a b -> p (a b)")[:, 0:3 * HD]]
        wk_raw = heads_out[:, :, :].rearrange("p a b -> p (a b)")[:, 0:KT * HOPS * D].rearrange(
            "p (t k d) -> p t k d", t=KT, k=HOPS)
        wout_raw = mix
        wv_raw = hop1[:, 0:KT, :]
        wv1_t = hop1[:, KT:2 * KT, :]
        wvh = value[:, 0:KT, :]
        wvh_t = hop0
        wmix_raw = y[:, 0:KT, :]
        bk_raw = hop1_full[:, 0:HOPS, :]
        small = scores[:, 0, :]
        att_cols = small[:, 0:4].rearrange("p (g o) -> p g o", o=1)
        bv_cols = small[:, 4:6].rearrange("p (g o) -> p g o", o=1)
        att_pairs = small[:, 6:10].rearrange("p (t o) -> p t o", t=KT)
        att_b_all = small[:, 10:11]
        att_proj = small[:, 12:16].rearrange("p (t o) -> p t o", t=KT)
        bv_proj = small[:, 16:18]
        bv_rep = leaky[:, 0, 0:KT * P].rearrange("p (t m) -> p t m", t=KT)
        src_rep = leaky[:, 1, 0:KT * P].rearrange("p (t m) -> p t m", t=KT)
        mask_rows_u8 = mask_in[0:B * NT, 0:P]
        mask_rows = scores[0:B * NT, 1, 0:P]

        bank = [ctx.enter_context(nc.psum_tensor(f"job_bank{i}", [P, 512], F32)) for i in range(RING)]
        score_bank = [ctx.enter_context(nc.psum_tensor(f"score_bank{i}", [P, 512], F32)) for i in range(2)]
        probs_bank = [ctx.enter_context(nc.psum_tensor(f"probs_bank{i}", [P, 512], F32)) for i in range(2)]
        out_bank = ctx.enter_context(nc.psum_tensor("out_bank", [P, 2 * NT, DH], F32))

        split_tiles = {"x_transpose": (x_hi, x_lo), "x1_transpose": (x1_hi, x1_lo),
                       "query": (q_hi, q_lo), "key": (k_hi, k_lo)}

        n_split0 = len(FIRST.split)
        n_split = len(FULL.split)
        x_loaded = every("x_loaded", 1)
        adj_loaded = every("adj_loaded", 1)
        mask_loaded = every("mask_loaded", 1)
        mask_read = every("mask_read", 1)
        job_done = Signal(sem("job_done"), len(FIRST.jobs), len(FULL.jobs))
        high_written = Signal(sem("high_written"), n_split0, n_split)
        split_written = Signal(sem("split_written"), n_split0, n_split)
        x_bias_written = every("x_bias_written", 1)
        value_written = every("value_written", NT)
        row_masks_written = every("row_masks_written", 1)
        mask_scaled = every("mask_scaled", 1)
        scores_done = every("scores_done", UNITS)
        max_written = every("max_written", UNITS)
        exp_bias_written = every("exp_bias_written", UNITS)
        probs_written = every("probs_written", UNITS)
        probs_turned = every("probs_turned", UNITS)
        probs_t_even = every("probs_t_even", UNITS // 2)
        probs_t_odd = every("probs_t_odd", UNITS // 2)
        head_done = every("head_done", HEADS)
        inv_written = every("inv_written", HEADS)
        head_normed = every("head_normed", HEADS)
        mixed_written = every("mixed_written", KT)
        adj_t_written = every("adj_t_written", NT)
        edge_exp_written = every("edge_exp_written", NT)
        edge_written = every("edge_written", NT)
        adj_part_written = every("adj_part_written", 2)
        heads_t_written = every("heads_t_written", NT)
        mix_written = every("mix_written", 2)
        moments0 = every("moments0", 2 * NT + 1)
        rstd0_written = every("rstd0_written", 1)
        x1_written = every("x1_written", NT)
        hop0_written = layer1_only("hop0_written", NT)
        edge_score_written = layer1_only("edge_score_written", NT)
        leaky_written = layer1_only("leaky_written", NT)
        alpha_exp_written = layer1_only("alpha_exp_written", NT)
        alpha_written = layer1_only("alpha_written", NT)
        hop12_written = layer1_only("hop12_written", NT)
        alpha_sum_written = layer1_only("alpha_sum_written", NT)
        alpha_inv_written = layer1_only("alpha_inv_written", NT)
        hop1_written = layer1_only("hop1_written", NT)
        hops_summed = layer1_only("hops_summed", NT)
        y_written = layer1_only("y_written", NT)
        moments1 = layer1_only("moments1", 2 * NT + 1)
        rstd1_written = layer1_only("rstd1_written", 1)
        out_written = layer1_only("out_written", 1)
        out_stored = every("out_stored", 1)

        wqkv_loaded = sem("wqkv_loaded")
        wk_loaded = sem("wk_loaded")
        small_loaded = sem("small_loaded")
        wout_loaded = sem("wout_loaded")
        wv_loaded = sem("wv_loaded")
        mask_rows_loaded = sem("mask_rows_loaded")
        const_written = sem("const_written")
        ident_written = sem("ident_written")
        setup_act = sem("setup_act")
        setup_dve = sem("setup_dve")
        setup_pe = sem("setup_pe")
        setup_hi = sem("setup_hi")

        def f32(t):
            return t.bitcast(F32)

        def halves(b):
            return b[:, :].rearrange("p (a d) -> p a d", a=2)

        block = ctx.enter_context(nc.Block())

        @block.sync
        def _(sp):
            for t in range(KT):
                sp.dma_start(wqkv_raw[t], w_qkv[t * P:(t + 1) * P, :]).then_inc(wqkv_loaded, 16)
            sp.dma_start(wout_raw[:, :, :], w_out.rearrange("(t p) d -> p t d", p=P)).then_inc(wout_loaded, 16)
            sp.dma_start(wv_raw, w_v.rearrange("(t p) d -> p t d", p=P)).then_inc(wv_loaded, 16)
            for t in range(KT):
                sp.dma_start(wk_raw[:, t, :, :], w_k[:, t * P:(t + 1) * P, :].rearrange("k p d -> p k d")
                             ).then_inc(wk_loaded, 16)
            sp.dma_start(att_cols, att_w.rearrange("(g p) o -> p g o", p=P), allow_slow_non_contiguous=True
                         ).then_inc(small_loaded, 16)
            sp.dma_start(bv_cols, b_v.rearrange("(g p o) -> p g o", p=P, o=1), allow_slow_non_contiguous=True
                         ).then_inc(small_loaded, 16)
            sp.dma_start(att_b_all, att_b.rearrange("(a o) -> a o", a=1).broadcast_to([P, 1])
                         ).then_inc(small_loaded, 16)
            sp.dma_start(b_out_all[:, :], b_out.rearrange("(a d) -> a d", a=1).broadcast_to([P, D])
                         ).then_inc(small_loaded, 16)
            sp.dma_start(bk_raw, b_k.rearrange("(a k) d -> a k d", a=1).broadcast_to([P, HOPS, D])
                         ).then_inc(small_loaded, 16)
            sp.dma_start(mask_rows_u8, nodemask.rearrange("b (t p) -> (b t) p", p=P)
                         ).then_inc(mask_rows_loaded, 16)

            def loaded_once():
                sp.wait_ge(wqkv_loaded, 16 * KT)

            def load_graph(s, plan):
                loaded_once()
                if not isinstance(s, int) or s > 0:
                    last = plan.order["x_transpose", KT - 1] + 1
                    job_done.wait(sp, s - 1, last)
                    x_bias_written.wait(sp, s - 1, 1)
                rows = x[bass.ds(s, 1)].rearrange("b (t p) d -> p (b t) d", p=P)
                sp.dma_start(x_in[:, :, :], rows).then_inc(x_loaded.sem, 16)
                loaded_once()
                if not isinstance(s, int) or s > 0:
                    mask_read.wait(sp, s - 1, 1)
                else:
                    sp.wait_ge(setup_dve, MASK_ROWS_STEP)
                sp.dma_start(mask_in[:, :], nodemask[bass.ds(s, 1)].broadcast_to([P, N])
                             ).then_inc(mask_loaded.sem, 16)
                loaded_once()
                if not isinstance(s, int) or s > 0:
                    job_done.wait(sp, s - 1, plan.order["adj_transpose", NT - 1] + 1)
                sp.dma_start(adj_in[:, :, :], adj[bass.ds(s, 1)].rearrange("b (t p) n -> p (b t) n", p=P)
                             ).then_inc(adj_loaded.sem, 16)

            def store_graph(s, g):
                loaded_once()
                out_written.wait(sp, s, 1)
                sp.dma_start(out[bass.ds(g, 1)].rearrange("b (t p) d -> p (b t) d", p=P), y[:, :, :]
                             ).then_inc(out_stored.sem, 16)

            sp.sem_inc(out_stored.sem, 16)
            load_graph(0, FIRST)
            load_graph(1, FIRST)
            with sp.Fori(2, B) as s:
                load_graph(s, FULL)
                store_graph(s - 1, s - 2)
            store_graph(B - 1, B - 2)
            store_graph(B, B - 1)
            out_stored.wait(sp, B, 1, 16)

        @block.tensor
        def _(pe):
            def split_product(dst, pairs, first=True):
                for n, (a_hi, a_lo, b_hi, b_lo) in enumerate(pairs):
                    nc.tensor.matmul(dst, a_hi, b_hi, start=(n == 0), stop=False)
                    nc.tensor.matmul(dst, a_hi, b_lo, start=False, stop=False)
                    last = nc.tensor.matmul(dst, a_lo, b_hi, start=False, stop=(n == len(pairs) - 1))
                return last

            pe.wait_ge(ident_written, 1)
            pe.wait_ge(setup_dve, MASK_ROWS_STEP)
            nc.tensor.transpose(bank[0][:, 0:B * NT], mask_rows, ident[0:B * NT, 0:B * NT]).then_inc(setup_pe, 1)
            pe.wait_ge(setup_act, 2)
            for t in range(HT):
                for c in range(KT):
                    last = nc.tensor.transpose(
                        bank[1 + t // 2][:, (t % 2) * D + c * P:(t % 2) * D + (c + 1) * P],
                        wvh[:, c, t * P:(t + 1) * P], ident[:, :])
            last.then_inc(setup_pe, 1)
            pe.wait_ge(wv_loaded, 16)
            for t in range(KT):
                for c in range(KT):
                    last = nc.tensor.transpose(score_bank[0][:, t * D + c * P:t * D + (c + 1) * P],
                                               wv_raw[:, c, t * P:(t + 1) * P], ident[:, :])
            last.then_inc(setup_pe, 1)
            pe.wait_ge(setup_dve, PROJ_READY_STEP)
            for c in range(KT):
                for t in range(HT):
                    last = nc.tensor.matmul(score_bank[1][:, c * D:(c + 1) * D], wvh_t[:, t, c * P:(c + 1) * P],
                                            wout[:, t, :], start=(t == 0), stop=(t == HT - 1))
            last.then_inc(setup_pe, 1)
            for c in range(KT):
                for t in range(KT):
                    last = nc.tensor.matmul(probs_bank[0][:, 2 * c:2 * c + 2], wv1_t[:, t, c * P:(c + 1) * P],
                                            att_pairs[:, t, :], start=(t == 0), stop=(t == KT - 1))
            for t in range(KT):
                last = nc.tensor.matmul(probs_bank[1][:, 0:2], bv_rep[:, t, :], att_pairs[:, t, :],
                                        start=(t == 0), stop=(t == KT - 1))
            last.then_inc(setup_pe, 1)
            pe.wait_ge(setup_dve, SETUP_DVE_STEPS)

            bank_read = {
                **{name: (lambda j, plan, name=name: (split_written, plan.split[name, j] + 1)) for name in SPLIT_JOBS},
                "value": lambda j, plan: (value_written, j + 1),
                "mixed_value": lambda j, plan: (mixed_written, j + 1),
                "adj_transpose": lambda j, plan: (edge_exp_written, j + 1),
                "adj_product": lambda j, plan: (adj_part_written, j + 1),
                "head_transpose": lambda j, plan: (heads_t_written, j + 1),
                "out_product": lambda j, plan: (mix_written, j + 1),
                "hop0": lambda j, plan: (hop0_written, j + 1),
                "source_score": lambda j, plan: (edge_score_written, NT),
                "hop12": lambda j, plan: (hop12_written, j + 1),
                "diffuse2": lambda j, plan: (hop1_written, j + 1),
                "diffuse1": lambda j, plan: (hops_summed, 2 * j + 2),
            }

            def begin(plan, s, name, index):
                n = plan.order[name, index] - RING
                if n >= 0:
                    _, old_name, old_index = plan.jobs[n]
                    signal, count = bank_read[old_name](old_index, plan)
                    signal.wait(pe, s, count)
                elif not isinstance(s, int) or s > 0:
                    _, old_name, old_index = LAYER0_JOBS[n]
                    signal, count = bank_read[old_name](old_index, plan)
                    signal.wait(pe, s - 1, count)
                return bank[plan.bank[name, index]]

            def job(plan, s, name, index):
                done = job_done.sem
                b = begin(plan, s, name, index)
                if name in ("x_transpose", "x1_transpose"):
                    if name == "x_transpose":
                        if index == 0:
                            x_loaded.wait(pe, s, 1, 16)
                        src = x_in
                    else:
                        if index == 0:
                            x1_written.wait(pe, s, 0)
                        src = x1
                    for t in range(NT):
                        last = nc.tensor.transpose(b[:, t * P:(t + 1) * P], src[:, t, index * P:(index + 1) * P],
                                                   ident[:, :])
                    last.then_inc(done, 1)
                elif name in ("query", "key"):
                    if index == 0:
                        split_written.wait(pe, s, plan.split["x_transpose", KT - 1] + 1)
                    kind = 0 if name == "query" else 1
                    cols = slice(index * P, (index + 1) * P)
                    split_product(b[:, :], [(wqkv_hi[:, t, kind, cols], wqkv_lo[:, t, kind, cols],
                                             x_hi[:, t, :], x_lo[:, t, :]) for t in range(KT)]).then_inc(done, 1)
                elif name == "value":
                    rows = slice(index * P, (index + 1) * P)
                    split_product(b[:, :], [(x_hi[:, t, rows], x_lo[:, t, rows],
                                             wqkv_hi[:, t, 2, :], wqkv_lo[:, t, 2, :]) for t in range(KT)]
                                  ).then_inc(done, 1)
                elif name == "mixed_value":
                    for half in range(2):
                        j = 2 * index + half
                        rows = slice(j * P, (j + 1) * P)
                        last = split_product(b[:, half * D:(half + 1) * D],
                                             [(x_hi[:, t, rows], x_lo[:, t, rows], wmix_hi[:, t, :], wmix_lo[:, t, :])
                                              for t in range(KT)])
                    last.then_inc(done, 1)
                elif name == "adj_transpose":
                    if index == 0:
                        adj_loaded.wait(pe, s, 1, 16)
                    for t in range(NT):
                        last = nc.tensor.transpose(b[:, t * P:(t + 1) * P], adj_in[:, t, index * P:(index + 1) * P],
                                                   ident[:, :])
                    last.then_inc(done, 1)
                elif name == "adj_product":
                    if index == 0:
                        edge_written.wait(pe, s, NT)
                        mixed_written.wait(pe, s, KT)
                    for half in range(2):
                        rows = slice((2 * index + half) * P, (2 * index + half + 1) * P)
                        for j in range(NT):
                            last = nc.tensor.matmul(b[:, half * D:(half + 1) * D], edge[:, j, rows], mixed[:, j, :],
                                                    start=(j == 0), stop=(j == NT - 1))
                    last.then_inc(done, 1)
                elif name == "head_transpose":
                    if index == 0:
                        head_normed.wait(pe, s, HEADS)
                    for t in range(HT):
                        last = nc.tensor.transpose(b[:, t * P:(t + 1) * P], heads_out[:, index, t * P:(t + 1) * P],
                                                   ident[:, :])
                    last.then_inc(done, 1)
                elif name == "out_product":
                    for half in range(2):
                        heads_t_written.wait(pe, s, 2 * index + half + 1)
                        for t in range(HT):
                            last = nc.tensor.matmul(b[:, half * D:(half + 1) * D],
                                                    heads_t[:, half, t * P:(t + 1) * P], wout[:, t, :],
                                                    start=(t == 0), stop=(t == HT - 1))
                    last.then_inc(done, 1)
                elif name == "hop0":
                    if index == 0:
                        split_written.wait(pe, s, plan.split["x1_transpose", KT - 1] + 1)
                    rows = slice(index * P, (index + 1) * P)
                    split_product(b[:, 0:D + 2], [(x1_hi[:, t, rows], x1_lo[:, t, rows], w0_hi[:, t, :], w0_lo[:, t, :])
                                                  for t in range(KT)]).then_inc(done, 1)
                elif name == "source_score":
                    split_product(b[:, :], [(wsrc_hi[:, t, :], wsrc_lo[:, t, :], x1_hi[:, t, :], x1_lo[:, t, :])
                                            for t in range(KT)]).then_inc(done, 1)
                elif name == "hop12":
                    rows = slice(index * P, (index + 1) * P)
                    split_product(b[:, :], [(x1_hi[:, t, rows], x1_lo[:, t, rows], w12_hi[:, t, :], w12_lo[:, t, :])
                                            for t in range(KT)]).then_inc(done, 1)
                elif name == "diffuse2":
                    if index == 0:
                        hop12_written.wait(pe, s, NT)
                        alpha_written.wait(pe, s, NT)
                    rows = slice(index * P, (index + 1) * P)
                    for j in range(NT):
                        last = nc.tensor.matmul(b[:, 0:D + 2], alpha[:, j, rows], hop2[:, j, :],
                                                start=(j == 0), stop=(j == NT - 1))
                    last.then_inc(done, 1)
                elif name == "diffuse1":
                    if index == 0:
                        hop1_written.wait(pe, s, NT)
                    for half in range(2):
                        rows = slice((2 * index + half) * P, (2 * index + half + 1) * P)
                        for j in range(NT):
                            last = nc.tensor.matmul(b[:, half * D:(half + 1) * D], alpha[:, j, rows],
                                                    hop1_full[:, j, :], start=(j == 0), stop=(j == NT - 1))
                    last.then_inc(done, 1)

            def score(s, plan, u):
                h, i = divmod(u, NT)
                pair, rows = h // 2, slice((h % 2) * DH, (h % 2 + 1) * DH)
                if i == 0 and h % 2 == 0:
                    split_written.wait(pe, s, plan.split["key", pair] + 1)
                max_written.wait(pe, s, u - 1)
                tile = slice(i * P, (i + 1) * P)
                split_product(score_bank[u % 2][:, :],
                              [(q_hi[rows, pair % 2, tile], q_lo[rows, pair % 2, tile],
                                k_hi[rows, pair % 2, :], k_lo[rows, pair % 2, :])]).then_inc(scores_done.sem, 1)

            def turn(s, u):
                probs_written.wait(pe, s, u + 1)
                if u % 2 == 0:
                    probs_t_even.wait(pe, s, u // 2)
                else:
                    probs_t_odd.wait(pe, s, u // 2)
                for j in range(NT):
                    last = nc.tensor.transpose(probs_bank[u % 2][:, j * P:(j + 1) * P],
                                               probs[:, u % 2, j * P:(j + 1) * P], ident[:, :])
                last.then_inc(probs_turned.sem, 1)

            def weigh(s, u):
                h, i = divmod(u, NT)
                if u == 0:
                    value_written.wait(pe, s, NT)
                if i == 0:
                    head_normed.wait(pe, s, h)
                if u % 2 == 0:
                    probs_t_even.wait(pe, s, u // 2 + 1)
                else:
                    probs_t_odd.wait(pe, s, u // 2 + 1)
                for j in range(NT):
                    last = nc.tensor.matmul(out_bank[:, i, :], probs_t[:, u % 2, j * P:(j + 1) * P],
                                            value[:, j, h * DH:(h + 1) * DH], start=(j == 0), stop=(j == NT - 1))
                if i == NT - 1:
                    last.then_inc(head_done.sem, 1)

            def step(s, plan):
                for slot in range(-1, UNITS + 3):
                    if plan.layer0 and 0 <= slot < UNITS:
                        score(s, plan, slot)
                    for name, index in plan.slots.get(slot, []):
                        job(plan, s, name, index)
                    if plan.layer0 and 0 <= slot - 1 < UNITS:
                        turn(s, slot - 1)
                    if plan.layer0 and 0 <= slot - 2 < UNITS:
                        weigh(s, slot - 2)

            step(0, FIRST)
            with pe.Fori(1, B) as s:
                step(s, FULL)
            step(B, LAST)

        @block.scalar
        def _(act):
            for t in range(KT):
                act.wait_ge(wqkv_loaded, 16 * KT)
                cols = wqkv_raw[t].rearrange("p (h i d) -> p i h d", h=HEADS, i=3)
                nc.scalar.activation(wvh[:, t, :].rearrange("p (h d) -> p h d", h=HEADS), cols[:, 2], ACT.Copy
                                     ).then_inc(setup_act, 1)
            for t in range(KT):
                cols = wqkv_raw[t].rearrange("p (h i d) -> p i h d", h=HEADS, i=3)
                for i in range(3):
                    nc.scalar.activation(wqkv_hi[:, t, i, :].rearrange("p (h d) -> p h d", h=HEADS), cols[:, i],
                                         ACT.Copy).then_inc(setup_hi, 1)
            act.wait_ge(wk_loaded, 16 * KT)
            for t in range(KT):
                nc.scalar.activation(w12_hi[:, t, :].rearrange("p (k d) -> p k d", k=2), wk_raw[:, t, 1:3, :],
                                     ACT.Copy).then_inc(setup_hi, 1)
            for t in range(KT):
                act.wait_ge(setup_dve, ATT_PROJ_STEP)
                nc.scalar.activation(w0_hi[:, t, 0:D], wk_raw[:, t, 0, :], ACT.Copy).then_inc(setup_hi, 1)
                nc.scalar.activation(w0_hi[:, t, D:D + 2], att_proj[:, t, :], ACT.Copy).then_inc(setup_hi, 1)
                nc.scalar.activation(wsrc_hi[:, t, :], src_rep[:, t, :], ACT.Copy).then_inc(setup_hi, 1)
                nc.scalar.activation(wmix_hi[:, t, :], wmix_raw[:, t, :], ACT.Copy).then_inc(setup_hi, 1)
            act.wait_ge(setup_dve, SETUP_DVE_STEPS)

            def job(plan, s, name, index):
                b = bank[plan.bank[name, index]]
                ready = plan.order[name, index] + 1
                if name in SPLIT_JOBS:
                    job_done.wait(act, s, ready)
                    high, _ = split_tiles[name]
                    nc.scalar.activation(high[:, index % 2, :], b[:, :], ACT.Copy).then_inc(high_written.sem, 1)
                elif name == "value":
                    job_done.wait(act, s, ready)
                    nc.scalar.activation(value[:, index, :], b[:, :], ACT.Copy).then_inc(value_written.sem, 1)
                elif name == "adj_transpose":
                    job_done.wait(act, s, ready)
                    if index == 0 and plan.layer1:
                        alpha_written.wait(act, s, NT)
                    nc.scalar.activation(adj_t[:, index, :], b[:, :], ACT.Copy).then_inc(adj_t_written.sem, 1)
                    if index >= 2:
                        edge_written.wait(act, s, index - 1)
                    nc.scalar.activation(exps[:, index % 2, :], b[:, :], ACT.Exp, scale=-1.0
                                         ).then_inc(edge_exp_written.sem, 1)
                elif name == "head_transpose":
                    job_done.wait(act, s, ready)
                    nc.scalar.activation(heads_t[:, index % 2, :], b[:, :], ACT.Copy).then_inc(heads_t_written.sem, 1)
                elif name == "hop12":
                    job_done.wait(act, s, ready)
                    nc.scalar.activation(hop1[:, index, :], b[:, 0:D], ACT.Copy)
                    nc.scalar.activation(hop2[:, index, 0:D], b[:, D:2 * D], ACT.Copy).then_inc(hop12_written.sem, 1)
                elif name == "source_score":
                    job_done.wait(act, s, ready)
                    hop0_written.wait(act, s, NT)
                    for j in range(NT + 1):
                        if j < NT:
                            if j >= 2:
                                alpha_exp_written.wait(act, s, j - 1)
                            nc.scalar.activation(leaky[:, j % 2, :], b[:, :], ACT.Identity,
                                                 bias=target_score[:, j:j + 1]).then_inc(edge_score_written.sem, 1)
                        if j >= 1:
                            leaky_written.wait(act, s, j)
                            if j == 1:
                                edge_written.wait(act, s, 0)
                            if j >= 3:
                                alpha_written.wait(act, s, j - 2)
                            nc.scalar.activation(exps[:, (j - 1) % 2, :], leaky[:, (j - 1) % 2, :], ACT.Exp
                                                 ).then_inc(alpha_exp_written.sem, 1)


            def exponent(s, u):
                i = u % NT
                exp_bias_written.wait(act, s, u + 1)
                probs_turned.wait(act, s, u - 1)
                nc.scalar.activation(probs[:, u % 2, :], scores[:, u % 2, :], ACT.Exp,
                                     bias=exp_bias[:, u % 2:u % 2 + 1], scale=row_scale[:, i:i + 1],
                                     accum_out=row_sum[:, (u // NT) % 2, i:i + 1]).then_inc(probs_written.sem, 1)

            def copy_turned(s, u):
                probs_turned.wait(act, s, u + 1)
                nc.scalar.activation(probs_t[:, u % 2, :], probs_bank[u % 2][:, :], ACT.Copy
                                     ).then_inc(probs_t_even.sem, 1)

            def step(s, plan):
                for slot in range(-1, UNITS + 3):
                    if plan.layer0 and 0 <= slot < UNITS:
                        exponent(s, slot)
                    for name, index in plan.slots.get(slot, []):
                        job(plan, s, name, index)
                    if plan.layer0 and 0 <= slot - 1 < UNITS and (slot - 1) % 2 == 0:
                        copy_turned(s, slot - 1)

            step(0, FIRST)
            with act.Fori(1, B) as s:
                step(s, FULL)
            step(B, LAST)

        @block.vector
        def _(dve):
            setup = [0]

            def link(instruction):
                setup[0] += 1
                instruction.then_inc(setup_dve, 1)
                dve.wait_ge(setup_dve, setup[0])

            dve.wait_ge(mask_rows_loaded, 16)
            link(nc.vector.tensor_copy(mask_rows, mask_rows_u8))
            assert setup[0] == MASK_ROWS_STEP
            dve.wait_ge(small_loaded, 16 * 5)
            for t in range(KT):
                for o in range(2):
                    link(nc.vector.tensor_copy(att_pairs[:, t, o:o + 1], att_cols[:, o * KT + t, :]))
            dve.wait_ge(const_written, 1)
            for t in range(KT):
                link(nc.vector.tensor_scalar(bv_rep[:, t, :], ones[:, :], bv_cols[:, t, :], None, ALU.mult))
            dve.wait_ge(wout_loaded, 16)
            link(nc.vector.tensor_scalar(wout[:, :, :], wout_raw[:, :, :], GAIN, None, ALU.mult))
            dve.wait_ge(setup_pe, 1)
            link(nc.vector.tensor_copy(mask_col[:, :], bank[0][:, 0:B * NT]))
            dve.wait_ge(setup_pe, 2)
            for t in range(HT):
                link(nc.vector.tensor_copy(wvh_t[:, t, :], bank[1 + t // 2][:, (t % 2) * D:(t % 2 + 1) * D]))
            dve.wait_ge(setup_pe, 3)
            link(nc.vector.tensor_copy(wv1_t, score_bank[0][:, :].rearrange("p (t d) -> p t d", t=KT)))
            assert setup[0] == PROJ_READY_STEP
            dve.wait_ge(setup_pe, 4)
            link(nc.vector.tensor_copy(wmix_raw, score_bank[1][:, :].rearrange("p (t d) -> p t d", t=KT)))
            dve.wait_ge(setup_pe, 5)
            link(nc.vector.tensor_copy(att_proj, probs_bank[0][:, 0:2 * KT].rearrange("p (t o) -> p t o", t=KT)))
            link(nc.vector.tensor_copy(bv_proj, probs_bank[1][:, 0:2]))
            link(nc.vector.tensor_tensor(score_const[:, :], bv_proj[:, 0:1], bv_proj[:, 1:2], ALU.add))
            link(nc.vector.tensor_tensor(score_const[:, :], score_const[:, :], att_b_all, ALU.add))
            for t in range(KT):
                link(nc.vector.tensor_scalar(src_rep[:, t, :], ones[:, :], att_proj[:, t, 1:2], None, ALU.mult))
            assert setup[0] == ATT_PROJ_STEP
            hi = 0
            for t in range(KT):
                cols = wqkv_raw[t].rearrange("p (h i d) -> p i h d", h=HEADS, i=3)
                for i in range(3):
                    hi += 1
                    dve.wait_ge(setup_hi, hi)
                    link(nc.vector.tensor_tensor(
                        wqkv_lo[:, t, i, :].rearrange("p (h d) -> p h d", h=HEADS), cols[:, i],
                        f32(wqkv_hi[:, t, i, :]).rearrange("p (h d) -> p h d", h=HEADS), ALU.subtract))
            for t in range(KT):
                hi += 1
                dve.wait_ge(setup_hi, hi)
                link(nc.vector.tensor_tensor(w12_lo[:, t, :].rearrange("p (k d) -> p k d", k=2), wk_raw[:, t, 1:3, :],
                                             f32(w12_hi[:, t, :]).rearrange("p (k d) -> p k d", k=2), ALU.subtract))
            for t in range(KT):
                for lo, raw, high in ((w0_lo[:, t, 0:D], wk_raw[:, t, 0, :], w0_hi[:, t, 0:D]),
                                      (w0_lo[:, t, D:D + 2], att_proj[:, t, :], w0_hi[:, t, D:D + 2]),
                                      (wsrc_lo[:, t, :], src_rep[:, t, :], wsrc_hi[:, t, :]),
                                      (wmix_lo[:, t, :], wmix_raw[:, t, :], wmix_hi[:, t, :])):
                    hi += 1
                    dve.wait_ge(setup_hi, hi)
                    link(nc.vector.tensor_tensor(lo, raw, f32(high), ALU.subtract))
            link(nc.vector.tensor_tensor(bk_sum[:, :], bk_raw[:, 0, :], bk_raw[:, 1, :], ALU.add))
            link(nc.vector.tensor_tensor(bk_sum[:, :], bk_sum[:, :], bk_raw[:, 2, :], ALU.add))
            link(nc.vector.memset(hop2[:, :, D:D + 2], 1.0))
            link(nc.vector.memset(neg_half[:, :], -0.5))
            assert setup[0] == SETUP_DVE_STEPS, setup[0]

            def masks(s):
                probs_written.wait(dve, s, 0)
                col = mask_col[:, bass.ds(s * NT, NT)]
                nc.vector.tensor_copy(row_mask[:, :], col)
                nc.vector.tensor_scalar(row_scale[:, :], col, SCORE_SCALE, None, ALU.mult)
                nc.vector.tensor_scalar(row_neg_scale[:, :], col, -SCORE_SCALE, None, ALU.mult
                                        ).then_inc(row_masks_written.sem, 1)
                mask_loaded.wait(dve, s, 1, 16)
                nc.vector.tensor_scalar(column_bias[:, :], mask_in[:, :], -1.0, MASKED, ALU.add, ALU.mult
                                        ).then_inc(mask_read.sem, 1)
                mask_read.wait(dve, s, 1)
                row_masks_written.wait(dve, s, 1)

            def score_max(s, u):
                i = u % NT
                scores_done.wait(dve, s, u + 1)
                probs_written.wait(dve, s, u - 1)
                nc.vector.memset(wait_carrier[:, :], 0.0)
                nc.vector.tensor_tensor_reduce(
                    out=scores[:, u % 2, :], in0=score_bank[u % 2][:, :], in1=column_bias[:, :], scale=1.0,
                    scalar=LOWEST, op0=ALU.add, op1=ALU.max, accum_out=row_max[:, u % 2:u % 2 + 1]
                ).then_inc(max_written.sem, 1)
                max_written.wait(dve, s, u + 1)
                nc.vector.tensor_tensor(exp_bias[:, u % 2:u % 2 + 1], row_max[:, u % 2:u % 2 + 1],
                                        row_neg_scale[:, i:i + 1], ALU.mult).then_inc(exp_bias_written.sem, 1)

            def copy_turned(s, u):
                probs_turned.wait(dve, s, u + 1)
                nc.vector.tensor_copy(probs_t[:, u % 2, :], probs_bank[u % 2][:, :]).then_inc(probs_t_odd.sem, 1)

            def normalize(s, h):
                probs_written.wait(dve, s, NT * h + NT)
                nc.vector.reciprocal(row_inv[:, h % 2, :], row_sum[:, h % 2, :]).then_inc(inv_written.sem, 1)
                inv_written.wait(dve, s, h + 1)
                head_done.wait(dve, s, h + 1)
                nc.vector.tensor_tensor(
                    heads_out[:, :, h * DH:(h + 1) * DH], out_bank[:, 0:NT, :],
                    row_inv[:, h % 2, :].rearrange("p (t o) -> p t o", o=1).broadcast_to([P, NT, DH]), ALU.mult
                ).then_inc(head_normed.sem, 1)

            def moments(s, src, written, stats, mean, var, signal):
                for t in range(NT):
                    written(t)
                    nc.vector.bn_stats(stats[:, t, :], src[:, t, :]).then_inc(signal.sem, 1)
                signal.wait(dve, s, NT)
                nc.vector.memset(wait_carrier[:, :], 0.0)
                for t in range(NT):
                    nc.vector.bn_aggr(mean[:, t, :], stats[:, t, :]).then_inc(signal.sem, 1)
                signal.wait(dve, s, 2 * NT)
                nc.vector.tensor_scalar(var[:, :], mean[:, :, 1], EPS_NORM, None, ALU.add).then_inc(signal.sem, 1)

            def job(plan, s, name, index):
                b = bank[plan.bank[name, index]]
                ready = plan.order[name, index] + 1
                if name in SPLIT_JOBS:
                    n = plan.split[name, index]
                    high_written.wait(dve, s, n + 1)
                    high, low = split_tiles[name]
                    nc.vector.tensor_tensor(low[:, index % 2, :], b[:, :], f32(high[:, index % 2, :]), ALU.subtract).then_inc(split_written.sem, 1)
                elif name == "mixed_value":
                    job_done.wait(dve, s, ready)
                    for half in range(2):
                        j = 2 * index + half
                        last = nc.vector.tensor_scalar(mixed[:, j, :], b[:, half * D:(half + 1) * D],
                                                       row_mask[:, j:j + 1], None, ALU.mult)
                    last.then_inc(mixed_written.sem, 1)
                elif name == "adj_product":
                    job_done.wait(dve, s, ready)
                    x_bias_written.wait(dve, s, 1)
                    for half in range(2):
                        t = 2 * index + half
                        last = nc.vector.scalar_tensor_tensor(
                            out=mix[:, t, :], in0=b[:, half * D:(half + 1) * D], scalar=row_mask[:, t:t + 1],
                            in1=x_bias[:, t, :], op0=ALU.mult, op1=ALU.add)
                    last.then_inc(adj_part_written.sem, 1)
                elif name == "out_product":
                    job_done.wait(dve, s, ready)
                    adj_part_written.wait(dve, s, 2)
                    rows = slice(2 * index, 2 * index + 2)
                    nc.vector.tensor_tensor(mix[:, rows, :], halves(b), mix[:, rows, :], ALU.add
                                            ).then_inc(mix_written.sem, 1)
                    if index == 1:
                        moments(s, mix, lambda t: mix_written.wait(dve, s, 2), stats0, mean0, var0, moments0)
                        rstd0_written.wait(dve, s, 1)
                        for t in range(NT):
                            nc.vector.tensor_scalar(x1[:, t, :], mix[:, t, :], mean0[:, t, 0:1], rstd0[:, t:t + 1],
                                                    ALU.subtract, ALU.mult).then_inc(x1_written.sem, 1)
                elif name == "hop0":
                    job_done.wait(dve, s, ready)
                    nc.vector.tensor_tensor(hop0[:, index, :], b[:, 0:D], bk_sum[:, :], ALU.add)
                    nc.vector.tensor_tensor(target_score[:, index:index + 1], b[:, D:D + 1], score_const[:, :],
                                            ALU.add).then_inc(hop0_written.sem, 1)
                elif name == "source_score":
                    for j in range(NT):
                        edge_score_written.wait(dve, s, j + 1)
                        half = leaky[:, j % 2, :]
                        nc.vector.scalar_tensor_tensor(out=half, in0=half, scalar=SLOPE, in1=half,
                                                       op0=ALU.mult, op1=ALU.max).then_inc(leaky_written.sem, 1)
                elif name == "diffuse2":
                    job_done.wait(dve, s, ready)
                    nc.vector.tensor_scalar(alpha_sum[:, index:index + 1], b[:, D:D + 1], EPS_SUM, None, ALU.add
                                            ).then_inc(alpha_sum_written.sem, 1)
                    alpha_sum_written.wait(dve, s, index + 1)
                    nc.vector.reciprocal(alpha_inv[:, index:index + 1], alpha_sum[:, index:index + 1]
                                         ).then_inc(alpha_inv_written.sem, 1)
                    alpha_inv_written.wait(dve, s, index + 1)
                    nc.vector.scalar_tensor_tensor(
                        out=hop1_full[:, index, :], in0=b[:, 0:D], scalar=alpha_inv[:, index:index + 1],
                        in1=hop1[:, index, :], op0=ALU.mult, op1=ALU.add).then_inc(hop1_written.sem, 1)
                elif name == "diffuse1":
                    job_done.wait(dve, s, ready)
                    for half in range(2):
                        t = 2 * index + half
                        nc.vector.scalar_tensor_tensor(
                            out=hop0[:, t, :], in0=b[:, half * D:(half + 1) * D], scalar=alpha_inv[:, t:t + 1],
                            in1=hop0[:, t, :], op0=ALU.mult, op1=ALU.add).then_inc(hops_summed.sem, 1)
                    hops_summed.wait(dve, s, 2 * index + 2)
                    if index == 0:
                        out_stored.wait(dve, s, 0, 16)
                    for t in (2 * index, 2 * index + 1):
                        nc.vector.scalar_tensor_tensor(out=y[:, t, :], in0=hop0[:, t, :], scalar=0.0, in1=x1[:, t, :],
                                                       op0=ALU.max, op1=ALU.add).then_inc(y_written.sem, 1)
                    if index == 1:
                        moments(s, y, lambda t: y_written.wait(dve, s, t + 1), stats1, mean1, var1, moments1)
                        rstd1_written.wait(dve, s, 1)
                        for t in range(NT):
                            last = nc.vector.tensor_scalar(y[:, t, :], y[:, t, :], mean1[:, t, 0:1],
                                                           rstd1[:, t:t + 1], ALU.subtract, ALU.mult)
                        last.then_inc(out_written.sem, 1)

            def step(s, plan):
                if plan.layer0:
                    masks(s)
                for slot in range(-1, UNITS + 3):
                    if plan.layer0 and 0 <= slot < UNITS:
                        score_max(s, slot)
                    for name, index in plan.slots.get(slot, []):
                        job(plan, s, name, index)
                    if plan.layer0 and 0 <= slot - 1 < UNITS and (slot - 1) % 2 == 1:
                        copy_turned(s, slot - 1)
                    if plan.layer0 and slot % NT == 1 and 0 <= slot // NT - 1 < HEADS:
                        normalize(s, slot // NT - 1)

            step(0, FIRST)
            with dve.Fori(1, B) as s:
                step(s, FULL)
            step(B, LAST)

        @block.gpsimd
        def _(pool):
            nc.gpsimd.memset(ones[:, :], 1.0).then_inc(const_written, 1)
            pool.wait_ge(const_written, 1)
            nc.gpsimd.affine_select(out=ident[:, :], in_=ones[:, :], compare_op=ALU.is_equal, fill=0.0, base=0,
                                    pattern=[[-1, P]], channel_multiplier=1).then_inc(ident_written, 1)
            pool.wait_ge(small_loaded, 16 * 5)
            pool.wait_ge(setup_dve, SETUP_DVE_STEPS)

            def reciprocal_root(s, moments, rstd, var, signal):
                moments.wait(pool, s, 2 * NT + 1)
                nc.gpsimd.tensor_tensor(rstd[:, :], var[:, :], neg_half[:, :], ALU.pow).then_inc(signal.sem, 1)

            def step(s, plan):
                if plan.layer0:
                    x_loaded.wait(pool, s, 1, 16)
                    adj_part_written.wait(pool, s, 0)
                    for t in range(NT):
                        last = nc.gpsimd.tensor_tensor(x_bias[:, t, :], x_in[:, t, :], b_out_all[:, :], ALU.add)
                    last.then_inc(x_bias_written.sem, 1)
                if plan.layer1:
                    for j in range(NT):
                        alpha_exp_written.wait(pool, s, j + 1)
                        adj_t_written.wait(pool, s, 0)
                        nc.gpsimd.tensor_tensor(alpha[:, j, :], exps[:, j % 2, :], adj_t[:, j, :], ALU.mult
                                                ).then_inc(alpha_written.sem, 1)
                    reciprocal_root(s, moments1, rstd1, var1, rstd1_written)
                if plan.layer0:
                    for j in range(NT):
                        edge_exp_written.wait(pool, s, j + 1)
                        nc.gpsimd.tensor_tensor(edge[:, j, :], exps[:, j % 2, :], adj_t[:, j, :], ALU.add
                                                ).then_inc(edge_written.sem, 1)
                    reciprocal_root(s, moments0, rstd0, var0, rstd0_written)

            step(0, FIRST)
            with pool.Fori(1, B) as s:
                step(s, FULL)
            step(B, LAST)


MASK_ROWS_STEP = 1
PROJ_READY_STEP = MASK_ROWS_STEP + 4 + 2 + 1 + 1 + 4 + 1
ATT_PROJ_STEP = PROJ_READY_STEP + 1 + 2 + 2 + 2
SETUP_DVE_STEPS = ATT_PROJ_STEP + 6 + 2 + 8 + 2 + 2

_INS = ['x', 'adj', 'nodemask', 'L0_gnn_W_qkv', 'L0_gnn_W_out', 'L0_gnn_b_out', 'L1_gnn_Wv', 'L1_gnn_bv',
        'L1_gnn_aw', 'L1_gnn_ab', 'L1_gnn_Wk', 'L1_gnn_bk']


def kernel(**inputs):
    import numpy as _np
    import concourse.bacc as _bacc
    from concourse import mybir as _mybir
    from concourse.bass_utils import run_bass_kernel_spmd as _run

    nc = _bacc.Bacc("TRN2", target_bir_lowering=False, num_devices=1)
    arrays, args = {}, []
    for name in _INS:
        a = _np.ascontiguousarray(inputs[name])
        arrays[f"in_{name}_dram"] = a
        args.append(nc.dram_tensor(f"in_{name}_dram", a.shape, _mybir.dt.from_np(a.dtype), kind="ExternalInput").ap())
    shape = inputs["x"].shape
    args.append(nc.dram_tensor("out_0_dram", shape, _mybir.dt.float32, kind="ExternalOutput").ap())
    graph_layers(nc, *args)
    r = _run(nc, [arrays], core_ids=[0])
    return r.results[0]["out_0_dram"]
```

```python
from contextlib import ExitStack

import concourse.bass as bass
from concourse import mybir

P = 128
F32 = mybir.dt.float32
F32R = mybir.dt.float32r
BF16 = mybir.dt.bfloat16
U8 = mybir.dt.uint8
ALU = mybir.AluOpType
ACT = mybir.ActivationFunctionType

HEADS = 8
DH = 64
GAIN = 0.33
SCORE_SCALE = DH ** -0.5
SLOPE = 0.2
EPS_NORM = 1e-5
EPS_SUM = 1e-12
MASKED = 1e30
LOWEST = -3.0e38

NEXT_JOBS = [(30, "x_transpose", 0), (31, "x_transpose", 1), (32, "query", 0), (33, "key", 0)]
LAYER0_JOBS = [
    (0, "value", 0), (1, "value", 1), (2, "value", 2), (3, "value", 3),
    (5, "query", 1), (6, "key", 1), (13, "query", 2), (14, "key", 2), (18, "query", 3), (19, "key", 3),
    (24, "mixed_value", 0), (25, "mixed_value", 1),
    (27, "adj_transpose", 0), (28, "adj_transpose", 1), (29, "adj_transpose", 2), (30, "adj_transpose", 3),
    (34, "adj_product", 0), (35, "adj_product", 1), (36, "adj_product", 2), (36, "adj_product", 3),
    (37, "out_product", 0), (37, "out_product", 1)]
LAYER1_JOBS = [
    (4, "x1_transpose", 0), (4, "x1_transpose", 1),
    (7, "hop0", 0), (8, "hop0", 1), (9, "hop0", 2), (10, "hop0", 3), (11, "source_score", 0),
    (12, "hop12", 0), (15, "hop12", 1), (16, "hop12", 2), (17, "hop12", 3),
    (20, "diffuse2", 0), (21, "diffuse2", 1), (22, "diffuse2", 2), (23, "diffuse2", 3),
    (26, "diffuse1", 0), (27, "diffuse1", 1), (28, "diffuse1", 2), (29, "diffuse1", 3)]
LAYER0_SIDE = [(30, "edge_split", 0), (31, "edge_split", 1), (32, "edge_split", 2), (33, "edge_split", 3),
               (26, "head_split", 0), (27, "head_split", 1), (33, "head_split", 2), (36, "head_split", 3)]
LAYER1_SIDE = [(0, "moments0", 0), (1, "normalize0", 0),
               (12, "edge_score", 0), (12, "edge_score", 1), (13, "edge_score", 2), (13, "edge_score", 3),
               (13, "alpha_exp", 0), (14, "alpha_exp", 1), (15, "alpha_exp", 2), (16, "alpha_exp", 3),
               (15, "alpha_split", 0), (16, "alpha_split", 1), (17, "alpha_split", 2), (18, "alpha_split", 3),
               (25, "hop1_split", 0), (25, "hop1_split", 1), (36, "moments1", 0), (37, "normalize1", 0)]
SPLITS = ("x_transpose", "query", "key", "value", "mixed_value", "x1_transpose", "hop12",
          "edge_split", "head_split", "alpha_split", "hop1_split")
RING = 3
SLOTS = range(38)
UNITS_END = 32


class Plan:

    def __init__(self, layer0, layer1, following, offset):
        jobs = (LAYER0_JOBS if layer0 else []) + (LAYER1_JOBS if layer1 else []) + (NEXT_JOBS if following else [])
        side = (LAYER0_SIDE if layer0 else []) + (LAYER1_SIDE if layer1 else [])
        self.jobs = sorted(jobs, key=lambda j: j[0])
        self.layer0, self.layer1 = layer0, layer1
        self.slots = {slot: [j[1:] for j in self.jobs if j[0] == slot] for slot in SLOTS}
        self.side = {slot: [j[1:] for j in side if j[0] == slot] for slot in SLOTS}
        self.order = {j[1:]: n for n, j in enumerate(self.jobs)}
        self.bank = {j[1:]: (n + offset) % RING for n, j in enumerate(self.jobs)}
        self.taken = {slot: [] for slot in SLOTS}
        for slot, *j in self.jobs:
            self.taken[slot + 1 if slot < UNITS_END else slot].append(tuple(j))
        split = [j for slot in SLOTS for j in self.side[slot] + self.taken[slot] if j[0] in SPLITS]
        self.split = {j: n for n, j in enumerate(split)}


FULL = Plan(True, True, True, 0)
assert len(FULL.jobs) % RING == 0
FIRST = Plan(True, False, True, -len(LAYER0_JOBS + NEXT_JOBS))
BEFORE = Plan(False, False, True, -len(LAYER0_JOBS + 2 * NEXT_JOBS))
FINAL = Plan(True, True, False, 0)
LAST = Plan(False, True, False, len(FINAL.jobs))
BEFORE.previous, FIRST.previous, FULL.previous, FINAL.previous, LAST.previous = None, BEFORE, FULL, FULL, FINAL
assert [j[1:] for j in FIRST.jobs[-RING:]] == [j[1:] for j in FULL.jobs[-RING:]]
assert not any(j[1] in SPLITS for j in FULL.jobs[-RING:])


class Signal:

    def __init__(self, sem, before, first, full, last, final):
        self.sem, self.before, self.first, self.full, self.last, self.final = sem, before, first, full, last, final

    def total(self, step, count, unit=1):
        if isinstance(step, int):
            start = 0 if step < 0 else self.before
            start += self.first if step > 0 else 0
            start += (min(step, self.final) - 1) * self.full if step > 1 else 0
            start += self.last if step > self.final else 0
            return (start + count) * unit
        assert self.before + self.first + count > 0, "a wait on a register must be on a value above zero"
        return step * (self.full * unit) + (self.before + self.first - self.full + count) * unit

    def wait(self, eng, step, count, unit=1):
        value = self.total(step, count, unit)
        if not isinstance(value, int) or value > 0:
            eng.wait_ge(self.sem, value)


def graph_layers(nc, x, adj, nodemask, w_qkv, w_out, b_out, w_v, b_v, att_w, att_b, w_k, b_k, out):
    B, N, D = x.shape
    NT = N // P
    KT = D // P
    HD = HEADS * DH
    HT = HD // P
    PAIRS = HEADS // 2
    UNITS = HEADS * NT
    HOPS = w_k.shape[0]
    BUFS = 3
    assert UNITS == UNITS_END and NT == 4 and KT == 2 and HT == 4 and HOPS == 3 and N == 512

    ctx = ExitStack()
    with ctx:
        def sb(name, shape, dt=F32):
            return ctx.enter_context(nc.sbuf_tensor(name, shape, dt))

        def sem(name):
            return ctx.enter_context(nc.semaphore(name))

        def every(name, count):
            return Signal(sem(name), 0, count, count, count, B - 1)

        def layer1_only(name, count):
            return Signal(sem(name), 0, 0, count, count, B - 1)

        def planned(name, count):
            return Signal(sem(name), count(BEFORE), count(FIRST), count(FULL), count(FINAL), B - 1)

        x_in = sb("x_in", [P, NT, D])
        adj_in = sb("adj_in", [P, NT, N])
        mask_in = sb("mask_in", [P, N], U8)
        mix = sb("mix", [P, NT, D])
        x_hi, x_lo = sb("x_hi", [P, KT, N], F32R), sb("x_lo", [P, KT, N], F32R)
        q_hi, q_lo = sb("q_hi", [P, 2, N], F32R), sb("q_lo", [P, 2, N], F32R)
        k_hi, k_lo = sb("k_hi", [P, 2, N], F32R), sb("k_lo", [P, 2, N], F32R)
        value = sb("value", [P, NT, HEADS, 2, DH], F32R)
        mixed_hi, mixed_lo = sb("mixed_hi", [P, NT, D], F32R), sb("mixed_lo", [P, NT, D], F32R)
        column_bias = sb("column_bias", [P, N], BF16)
        row_mask = sb("row_mask", [P, NT])
        row_scale = sb("row_scale", [P, NT])
        row_neg_scale = sb("row_neg_scale", [P, NT])
        row_max = sb("row_max", [P, 2])
        exp_bias = sb("exp_bias", [P, 2])
        row_sum = sb("row_sum", [P, NT])
        row_inv = sb("row_inv", [P, NT])
        probs = sb("probs", [P, BUFS, N])
        turned_hi, turned_lo = sb("turned_hi", [P, NT, N], F32R), sb("turned_lo", [P, NT, N], F32R)
        heads = sb("heads", [P, HT, N])
        adj_t = sb("adj_t", [P, NT, N])
        edge_hi, edge_lo = sb("edge_hi", [P, NT, N], F32R), sb("edge_lo", [P, NT, N], F32R)
        edge = sb("edge", [P, 3, N])
        x1 = sb("x1", [P, NT, D])
        x1_hi, x1_lo = sb("x1_hi", [P, KT, N], F32R), sb("x1_lo", [P, KT, N], F32R)
        y = sb("y", [P, NT, D])
        hop1 = sb("hop1", [P, NT, D])
        hop_hi, hop_lo = sb("hop_hi", [P, NT, D + 2], F32R), sb("hop_lo", [P, NT, D + 2], F32R)
        target_score = sb("target_score", [P, NT])
        alpha_inv = sb("alpha_inv", [P, NT])
        alpha_sum = sb("alpha_sum", [P, NT])
        stats0, stats1 = sb("stats0", [P, NT, 6]), sb("stats1", [P, NT, 6])
        mean0, mean1 = sb("mean0", [P, NT, 2]), sb("mean1", [P, NT, 2])
        var0, var1 = sb("var0", [P, NT]), sb("var1", [P, NT])
        rstd0, rstd1 = sb("rstd0", [P, NT]), sb("rstd1", [P, NT])
        wait_carrier = sb("wait_carrier", [P, 1])

        ident = sb("ident", [P, P])
        neg_half = sb("neg_half", [P, NT])
        mask_col = sb("mask_col", [P, B * NT])
        wqkv_hi = sb("wqkv_hi", [P, KT, 3, HD], F32R)
        wqkv_lo = sb("wqkv_lo", [P, KT, 3, HD], F32R)
        wout_hi, wout_lo = sb("wout_hi", [P, HT, D], F32R), sb("wout_lo", [P, HT, D], F32R)
        wmix_hi, wmix_lo = sb("wmix_hi", [P, KT, D], F32R), sb("wmix_lo", [P, KT, D], F32R)
        w12_hi, w12_lo = sb("w12_hi", [P, KT, 2 * D], F32R), sb("w12_lo", [P, KT, 2 * D], F32R)
        w0_hi, w0_lo = sb("w0_hi", [P, KT, D + 2], F32R), sb("w0_lo", [P, KT, D + 2], F32R)
        wsrc_hi, wsrc_lo = sb("wsrc_hi", [P, KT, P], F32R), sb("wsrc_lo", [P, KT, P], F32R)
        b_out_all = sb("b_out_all", [P, D])
        bk_sum = sb("bk_sum", [P, D])
        score_const = sb("score_const", [P, 1])

        def flat(t):
            return t[:, :, :].rearrange("p a b -> p (a b)")

        wqkv_raw = [flat(adj_t)[:, 0:3 * HD], flat(adj_in)[:, 0:3 * HD]]
        wk_raw = flat(heads)[:, 0:KT * HOPS * D].rearrange("p (t k d) -> p t k d", t=KT, k=HOPS)
        ones = flat(heads)[:, KT * HOPS * D:KT * HOPS * D + P]
        ones_pairs = ones[:, 0:2 * NT].rearrange("p (t o) -> p t o", t=NT)
        wout = mix
        wv_raw = hop1[:, 0:KT, :]
        wv1_t = hop1[:, KT:2 * KT, :]
        wvh = flat(x1).rearrange("p (t n) -> p t n", t=KT)
        wvh_t = y
        wmix_raw = edge[:, 0, :].rearrange("p (t d) -> p t d", t=KT)
        bv_rep = edge[:, 1, 0:KT * P].rearrange("p (t m) -> p t m", t=KT)
        src_rep = edge[:, 1, KT * P:2 * KT * P].rearrange("p (t m) -> p t m", t=KT)
        bk_raw = flat(probs)[:, 0:HOPS * D].rearrange("p (k d) -> p k d", k=HOPS)
        small = probs[:, 2, :]
        att_cols = small[:, 0:4].rearrange("p (g o) -> p g o", o=1)
        bv_cols = small[:, 4:6].rearrange("p (g o) -> p g o", o=1)
        att_pairs = small[:, 6:10].rearrange("p (t o) -> p t o", t=KT)
        att_b_all = small[:, 10:11]
        att_proj = small[:, 12:16].rearrange("p (t o) -> p t o", t=KT)
        bv_proj = small[:, 16:18]
        mask_rows = small[0:B * NT, P:2 * P]
        mask_rows_u8 = mask_in[0:B * NT, 0:P]

        bank = [ctx.enter_context(nc.psum_tensor(f"job_bank{i}", [P, 512], F32)) for i in range(RING)]
        score_bank = [ctx.enter_context(nc.psum_tensor(f"score_bank{i}", [P, 512], F32)) for i in range(2)]
        turned_bank = [ctx.enter_context(nc.psum_tensor(f"turned_bank{i}", [P, 512], F32)) for i in range(2)]
        out_bank = ctx.enter_context(nc.psum_tensor("out_bank", [P, 512], F32))

        def edge_tile(layer, index):
            if index < 3:
                return edge[:, index, :]
            return heads[:, HT - 1, :] if layer == 1 else edge[:, 0, :]

        def parts(name, index):
            slot = index % 2
            rows2 = slice(2 * index, 2 * index + 2)
            return {
                "x_transpose": lambda: (x_hi[:, slot, :], x_lo[:, slot, :]),
                "x1_transpose": lambda: (x1_hi[:, slot, :], x1_lo[:, slot, :]),
                "query": lambda: (q_hi[:, slot, :], q_lo[:, slot, :]),
                "key": lambda: (k_hi[:, slot, :], k_lo[:, slot, :]),
                "value": lambda: (value[:, index, :, 0, :], value[:, index, :, 1, :]),
                "hop12": lambda: (hop_hi[:, index, 0:D], hop_lo[:, index, 0:D]),
                "hop1_split": lambda: (hop_hi[:, rows2, 0:D], hop_lo[:, rows2, 0:D]),
                "edge_split": lambda: (edge_hi[:, index, :], edge_lo[:, index, :]),
                "alpha_split": lambda: (edge_hi[:, index, :], edge_lo[:, index, :]),
                "head_split": lambda: (x1_hi[:, slot, :], x1_lo[:, slot, :]) if index < KT else
                                      (hop_hi[:, 2 * slot:2 * slot + 2, 0:D], hop_lo[:, 2 * slot:2 * slot + 2, 0:D]),
            }[name]()

        def head_rows(t, i):
            if t < KT:
                return x1_hi[:, t, i * P:(i + 1) * P], x1_lo[:, t, i * P:(i + 1) * P]
            cols = slice((i % 2) * P, (i % 2 + 1) * P)
            return tuple(part[:, 2 * (t - KT) + i // 2, cols] for part in (hop_hi, hop_lo))

        def whole(plan, name, index):
            if name == "hop1_split":
                return hop1[:, 2 * index:2 * index + 2, :]
            if name in ("edge_split", "alpha_split"):
                return edge_tile(0 if name == "edge_split" else 1, index)
            if name == "head_split":
                return heads[:, index, :] if index < KT else heads[:, index, :].rearrange("p (a d) -> p a d", a=2)
            b = bank[plan.bank[name, index]]
            if name == "hop12":
                return b[:, D:2 * D]
            if name == "value":
                return b[:, :].rearrange("p (h d) -> p h d", h=HEADS)
            return b[:, :]

        x_loaded = every("x_loaded", 1)
        adj_loaded = every("adj_loaded", 1)
        mask_loaded = every("mask_loaded", 1)
        mask_read = every("mask_read", 1)
        row_masks_written = every("row_masks_written", 1)
        x_bias_written = every("x_bias_written", 1)
        job_done = planned("job_done", lambda plan: len(plan.jobs))
        high_written = planned("high_written", lambda plan: len(plan.split))
        split_written = planned("split_written", lambda plan: len(plan.split))
        scores_done = every("scores_done", UNITS)
        max_written = every("max_written", UNITS)
        exp_bias_written = every("exp_bias_written", UNITS)
        exp_written = every("exp_written", UNITS)
        inv_written = every("inv_written", UNITS)
        probs_written = every("probs_written", UNITS)
        probs_turned = every("probs_turned", UNITS)
        turned_high = every("turned_high", UNITS)
        turned_split = every("turned_split", UNITS)
        half_done = every("half_done", 2 * HEADS)
        head_low_copied = every("head_low_copied", HEADS)
        head_written = every("head_written", HEADS)
        edge_exp_written = every("edge_exp_written", NT)
        edge_written = every("edge_written", NT)
        adj_part_written = every("adj_part_written", NT)
        mix_written = every("mix_written", 2)
        moments0 = layer1_only("moments0", 2 * NT + 1)
        rstd0_written = layer1_only("rstd0_written", 1)
        x1_written = layer1_only("x1_written", NT)
        hop0_written = layer1_only("hop0_written", NT)
        edge_score_written = layer1_only("edge_score_written", NT)
        leaky_written = layer1_only("leaky_written", NT)
        alpha_exp_written = layer1_only("alpha_exp_written", NT)
        alpha_written = layer1_only("alpha_written", NT)
        alpha_sum_written = layer1_only("alpha_sum_written", NT)
        alpha_inv_written = layer1_only("alpha_inv_written", NT)
        hop1_written = layer1_only("hop1_written", NT)
        hops_summed = layer1_only("hops_summed", NT)
        y_written = layer1_only("y_written", NT)
        moments1 = layer1_only("moments1", 2 * NT + 1)
        rstd1_written = layer1_only("rstd1_written", 1)
        out_written = layer1_only("out_written", 1)
        out_stored = every("out_stored", 1)

        wqkv_loaded = sem("wqkv_loaded")
        wk_loaded = sem("wk_loaded")
        small_loaded = sem("small_loaded")
        wout_loaded = sem("wout_loaded")
        wv_loaded = sem("wv_loaded")
        mask_rows_loaded = sem("mask_rows_loaded")
        const_written = sem("const_written")
        ident_written = sem("ident_written")
        setup_act = sem("setup_act")
        setup_dve = sem("setup_dve")
        setup_pe = sem("setup_pe")
        setup_hi = sem("setup_hi")

        def f32(t):
            return t.bitcast(F32)

        def halves(b):
            return b[:, :].rearrange("p (a d) -> p a d", a=2)

        block = ctx.enter_context(nc.Block())

        @block.sync
        def _(sp):
            for t in range(KT):
                sp.dma_start(wqkv_raw[t], w_qkv[t * P:(t + 1) * P, :]).then_inc(wqkv_loaded, 16)
            sp.dma_start(wout[:, :, :], w_out.rearrange("(t p) d -> p t d", p=P)).then_inc(wout_loaded, 16)
            sp.dma_start(wv_raw, w_v.rearrange("(t p) d -> p t d", p=P)).then_inc(wv_loaded, 16)
            for t in range(KT):
                sp.dma_start(wk_raw[:, t, :, :], w_k[:, t * P:(t + 1) * P, :].rearrange("k p d -> p k d")
                             ).then_inc(wk_loaded, 16)
            sp.dma_start(att_cols, att_w.rearrange("(g p) o -> p g o", p=P), allow_slow_non_contiguous=True
                         ).then_inc(small_loaded, 16)
            sp.dma_start(bv_cols, b_v.rearrange("(g p o) -> p g o", p=P, o=1), allow_slow_non_contiguous=True
                         ).then_inc(small_loaded, 16)
            sp.dma_start(att_b_all, att_b.rearrange("(a o) -> a o", a=1).broadcast_to([P, 1])
                         ).then_inc(small_loaded, 16)
            sp.dma_start(b_out_all[:, :], b_out.rearrange("(a d) -> a d", a=1).broadcast_to([P, D])
                         ).then_inc(small_loaded, 16)
            sp.dma_start(bk_raw, b_k.rearrange("(a k) d -> a k d", a=1).broadcast_to([P, HOPS, D])
                         ).then_inc(small_loaded, 16)
            sp.dma_start(mask_rows_u8, nodemask.rearrange("b (t p) -> (b t) p", p=P)
                         ).then_inc(mask_rows_loaded, 16)

            def loaded_once():
                sp.wait_ge(wqkv_loaded, 16 * KT)

            def load_graph(s, plan):
                loaded_once()
                if not isinstance(s, int) or s > 0:
                    job_done.wait(sp, s - 1, 0)
                    x_bias_written.wait(sp, s - 1, 1)
                rows = x[bass.ds(s, 1)].rearrange("b (t p) d -> p (b t) d", p=P)
                sp.dma_start(x_in[:, :, :], rows).then_inc(x_loaded.sem, 16)
                loaded_once()
                if not isinstance(s, int) or s > 0:
                    mask_read.wait(sp, s - 1, 1)
                else:
                    sp.wait_ge(setup_dve, MASK_ROWS_STEP)
                sp.dma_start(mask_in[:, :], nodemask[bass.ds(s, 1)].broadcast_to([P, N])
                             ).then_inc(mask_loaded.sem, 16)
                loaded_once()
                if not isinstance(s, int) or s > 0:
                    job_done.wait(sp, s - 1, plan.order["adj_transpose", NT - 1] + 1)
                else:
                    sp.wait_ge(setup_dve, SETUP_DVE_STEPS)
                sp.dma_start(adj_in[:, :, :], adj[bass.ds(s, 1)].rearrange("b (t p) n -> p (b t) n", p=P)
                             ).then_inc(adj_loaded.sem, 16)

            def store_graph(s, g):
                loaded_once()
                out_written.wait(sp, s, 1)
                sp.dma_start(out[bass.ds(g, 1)].rearrange("b (t p) d -> p (b t) d", p=P), y[:, :, :]
                             ).then_inc(out_stored.sem, 16)

            sp.sem_inc(out_stored.sem, 16)
            load_graph(0, FIRST)
            load_graph(1, FIRST)
            with sp.Fori(2, B) as s:
                load_graph(s, FULL)
                store_graph(s - 1, s - 2)
            store_graph(B - 1, B - 2)
            store_graph(B, B - 1)
            out_stored.wait(sp, B, 1, 16)

        @block.tensor
        def _(pe):
            def split_product(dst, pairs, first=True):
                for n, (a_hi, a_lo, b_hi, b_lo) in enumerate(pairs):
                    nc.tensor.matmul(dst, a_hi, b_hi, start=(n == 0), stop=False)
                    nc.tensor.matmul(dst, a_hi, b_lo, start=False, stop=False)
                    last = nc.tensor.matmul(dst, a_lo, b_hi, start=False, stop=(n == len(pairs) - 1))
                return last

            pe.wait_ge(ident_written, 1)
            pe.wait_ge(setup_dve, MASK_ROWS_STEP)
            nc.tensor.transpose(bank[0][:, 0:B * NT], mask_rows, ident[0:B * NT, 0:B * NT]).then_inc(setup_pe, 1)
            pe.wait_ge(setup_act, 2)
            for t in range(HT):
                for c in range(KT):
                    last = nc.tensor.transpose(
                        bank[1 + t // 2][:, (t % 2) * D + c * P:(t % 2) * D + (c + 1) * P],
                        wvh[:, c, t * P:(t + 1) * P], ident[:, :])
            last.then_inc(setup_pe, 1)
            pe.wait_ge(wv_loaded, 16)
            for t in range(KT):
                for c in range(KT):
                    last = nc.tensor.transpose(score_bank[0][:, t * D + c * P:t * D + (c + 1) * P],
                                               wv_raw[:, c, t * P:(t + 1) * P], ident[:, :])
            last.then_inc(setup_pe, 1)
            pe.wait_ge(setup_dve, PROJ_READY_STEP)
            for c in range(KT):
                for t in range(HT):
                    last = nc.tensor.matmul(score_bank[1][:, c * D:(c + 1) * D], wvh_t[:, t, c * P:(c + 1) * P],
                                            wout[:, t, :], start=(t == 0), stop=(t == HT - 1))
            last.then_inc(setup_pe, 1)
            for c in range(KT):
                for t in range(KT):
                    last = nc.tensor.matmul(turned_bank[0][:, 2 * c:2 * c + 2], wv1_t[:, t, c * P:(c + 1) * P],
                                            att_pairs[:, t, :], start=(t == 0), stop=(t == KT - 1))
            for t in range(KT):
                last = nc.tensor.matmul(turned_bank[1][:, 0:2], bv_rep[:, t, :], att_pairs[:, t, :],
                                        start=(t == 0), stop=(t == KT - 1))
            last.then_inc(setup_pe, 1)
            pe.wait_ge(setup_dve, SETUP_DVE_STEPS)

            def bank_read(plan, name, index):
                if name in SPLITS:
                    return split_written, plan.split[name, index] + 1
                return {"adj_transpose": edge_exp_written, "adj_product": adj_part_written,
                        "out_product": mix_written, "hop0": hop0_written, "source_score": edge_score_written,
                        "diffuse2": hop1_written, "diffuse1": hops_summed
                        }[name], NT if name == "source_score" else index + 1

            def begin(plan, s, name, index):
                n = plan.order[name, index] - RING
                if n >= 0:
                    signal, count = bank_read(plan, *plan.jobs[n][1:])
                    signal.wait(pe, s, count)
                elif plan.previous and -n <= len(plan.previous.jobs):
                    signal, count = bank_read(plan.previous, *plan.previous.jobs[n][1:])
                    signal.wait(pe, s - 1, count)
                return bank[plan.bank[name, index]]

            def split_ready(plan, s, name, index):
                split_written.wait(pe, s, plan.split[name, index] + 1)

            def tile(index):
                return slice(index * P, (index + 1) * P)

            def job(plan, s, name, index):
                done = job_done.sem
                b = begin(plan, s, name, index)
                if name in ("x_transpose", "x1_transpose", "adj_transpose"):
                    if index == 0:
                        if name == "x_transpose":
                            x_loaded.wait(pe, s + 1, 1, 16)
                        elif name == "adj_transpose":
                            adj_loaded.wait(pe, s, 1, 16)
                        else:
                            x1_written.wait(pe, s, NT)
                    src = {"x_transpose": x_in, "x1_transpose": x1, "adj_transpose": adj_in}[name]
                    for t in range(NT):
                        last = nc.tensor.transpose(b[:, tile(t)], src[:, t, tile(index)], ident[:, :])
                elif name in ("query", "key"):
                    if index == 0:
                        split_ready(plan, s, "x_transpose", KT - 1)
                    kind = 0 if name == "query" else 1
                    last = split_product(b[:, :], [(wqkv_hi[:, t, kind, tile(index)], wqkv_lo[:, t, kind, tile(index)],
                                                    x_hi[:, t, :], x_lo[:, t, :]) for t in range(KT)])
                elif name == "value":
                    if index == 0:
                        split_written.wait(pe, s, 0)
                    last = split_product(b[:, :], [(x_hi[:, t, tile(index)], x_lo[:, t, tile(index)],
                                                    wqkv_hi[:, t, 2, :], wqkv_lo[:, t, 2, :]) for t in range(KT)])
                elif name == "mixed_value":
                    for half in range(2):
                        rows = tile(2 * index + half)
                        last = split_product(b[:, half * D:(half + 1) * D],
                                             [(x_hi[:, t, rows], x_lo[:, t, rows], wmix_hi[:, t, :], wmix_lo[:, t, :])
                                              for t in range(KT)])
                elif name == "adj_product":
                    if index == 0:
                        split_ready(plan, s, "edge_split", NT - 1)
                        split_ready(plan, s, "mixed_value", 1)
                    last = split_product(b[:, 0:D], [(edge_hi[:, j, tile(index)], edge_lo[:, j, tile(index)],
                                                      mixed_hi[:, j, :], mixed_lo[:, j, :]) for j in range(NT)])
                elif name == "out_product":
                    if index == 0:
                        split_ready(plan, s, "head_split", HT - 1)
                    for half in range(2):
                        last = split_product(b[:, half * D:(half + 1) * D],
                                             [head_rows(t, 2 * index + half)
                                              + (wout_hi[:, t, :], wout_lo[:, t, :]) for t in range(HT)])
                elif name == "hop0":
                    if index == 0:
                        split_ready(plan, s, "x1_transpose", KT - 1)
                    last = split_product(b[:, 0:D + 2], [(x1_hi[:, t, tile(index)], x1_lo[:, t, tile(index)],
                                                          w0_hi[:, t, :], w0_lo[:, t, :]) for t in range(KT)])
                elif name == "source_score":
                    last = split_product(b[:, :], [(wsrc_hi[:, t, :], wsrc_lo[:, t, :], x1_hi[:, t, :], x1_lo[:, t, :])
                                                   for t in range(KT)])
                elif name == "hop12":
                    last = split_product(b[:, :], [(x1_hi[:, t, tile(index)], x1_lo[:, t, tile(index)],
                                                    w12_hi[:, t, :], w12_lo[:, t, :]) for t in range(KT)])
                elif name == "diffuse2":
                    if index == 0:
                        split_ready(plan, s, "hop12", NT - 1)
                        split_ready(plan, s, "alpha_split", NT - 1)
                    last = split_product(b[:, 0:D + 2], [(edge_hi[:, j, tile(index)], edge_lo[:, j, tile(index)],
                                                          hop_hi[:, j, :], hop_lo[:, j, :]) for j in range(NT)])
                elif name == "diffuse1":
                    if index == 0:
                        split_ready(plan, s, "hop1_split", 1)
                    last = split_product(b[:, 0:D], [(edge_hi[:, j, tile(index)], edge_lo[:, j, tile(index)],
                                                      hop_hi[:, j, 0:D], hop_lo[:, j, 0:D]) for j in range(NT)])
                last.then_inc(done, 1)

            def score(s, plan, u):
                h, i = divmod(u, NT)
                pair, rows = h // 2, slice((h % 2) * DH, (h % 2 + 1) * DH)
                if u == 0:
                    split_written.wait(pe, s, 0)
                elif i == 0 and h % 2 == 0:
                    split_ready(plan, s, "key", pair)
                max_written.wait(pe, s, u - 1)
                split_product(score_bank[u % 2][:, :],
                              [(q_hi[rows, pair % 2, tile(i)], q_lo[rows, pair % 2, tile(i)],
                                k_hi[rows, pair % 2, :], k_lo[rows, pair % 2, :])]).then_inc(scores_done.sem, 1)

            def turn(s, u):
                probs_written.wait(pe, s, u + 1)
                turned_split.wait(pe, s, u - 1)
                for j in range(NT):
                    last = nc.tensor.transpose(turned_bank[u % 2][:, tile(j)], probs[:, u % BUFS, tile(j)], ident[:, :])
                last.then_inc(probs_turned.sem, 1)

            def weigh(s, plan, h, half):
                if h == 0 and half == 0:
                    split_ready(plan, s, "value", NT - 1)
                if half == 0:
                    head_written.wait(pe, s, h)
                turned_split.wait(pe, s, NT * h + 2 * half + 2)
                cols = slice(half * 2 * P, (half + 1) * 2 * P)
                for j in range(NT):
                    both = value[:, j, h, :, :].rearrange("p a d -> p (a d)")
                    nc.tensor.matmul(out_bank[:, cols], both, turned_hi[:, j, cols], start=(j == 0), stop=False)
                    last = nc.tensor.matmul(out_bank[:, cols], both, turned_lo[:, j, cols], start=False,
                                            stop=(j == NT - 1))
                last.then_inc(half_done.sem, 1)

            def step(s, plan):
                for slot in SLOTS:
                    if plan.layer0 and 0 <= slot < UNITS:
                        score(s, plan, slot)
                    h, half = divmod(slot - 5, NT)
                    if plan.layer0 and half % 2 == 0 and 0 <= h < HEADS:
                        weigh(s, plan, h, half // 2)
                    for name, index in plan.slots[slot]:
                        job(plan, s, name, index)
                    if plan.layer0 and 0 <= slot - 2 < UNITS:
                        turn(s, slot - 2)

            step(-1, BEFORE)
            step(0, FIRST)
            with pe.Fori(1, B - 1) as s:
                step(s, FULL)
            step(B - 1, FINAL)
            step(B, LAST)

        @block.scalar
        def _(act):
            for t in range(KT):
                act.wait_ge(wqkv_loaded, 16 * KT)
                cols = wqkv_raw[t].rearrange("p (h i d) -> p i h d", h=HEADS, i=3)
                nc.scalar.activation(wvh[:, t, :].rearrange("p (h d) -> p h d", h=HEADS), cols[:, 2], ACT.Copy
                                     ).then_inc(setup_act, 1)
            for t in range(KT):
                cols = wqkv_raw[t].rearrange("p (h i d) -> p i h d", h=HEADS, i=3)
                for i in range(3):
                    nc.scalar.activation(wqkv_hi[:, t, i, :].rearrange("p (h d) -> p h d", h=HEADS), cols[:, i],
                                         ACT.Copy).then_inc(setup_hi, 1)
            act.wait_ge(wk_loaded, 16 * KT)
            for t in range(KT):
                nc.scalar.activation(w12_hi[:, t, :].rearrange("p (k d) -> p k d", k=2), wk_raw[:, t, 1:3, :],
                                     ACT.Copy).then_inc(setup_hi, 1)
            for t in range(KT):
                act.wait_ge(setup_dve, ATT_PROJ_STEP)
                nc.scalar.activation(w0_hi[:, t, 0:D], wk_raw[:, t, 0, :], ACT.Copy).then_inc(setup_hi, 1)
                nc.scalar.activation(w0_hi[:, t, D:D + 2], att_proj[:, t, :], ACT.Copy).then_inc(setup_hi, 1)
                nc.scalar.activation(wsrc_hi[:, t, :], src_rep[:, t, :], ACT.Copy).then_inc(setup_hi, 1)
                nc.scalar.activation(wmix_hi[:, t, :], wmix_raw[:, t, :], ACT.Copy).then_inc(setup_hi, 1)
            for t in range(HT):
                nc.scalar.activation(wout_hi[:, t, :], wout[:, t, :], ACT.Copy).then_inc(setup_hi, 1)
            act.wait_ge(setup_dve, SETUP_DVE_STEPS)

            def split(plan, s, name, index):
                if name in plan_banks:
                    job_done.wait(act, s, plan.order[name, index] + 1)
                elif name == "edge_split":
                    edge_written.wait(act, s, index + 1)
                    if index == 0 and plan.layer1:
                        job_done.wait(act, s, plan.order["diffuse1", NT - 1] + 1)
                elif name == "alpha_split":
                    alpha_written.wait(act, s, index + 1)
                elif name == "hop1_split":
                    hop1_written.wait(act, s, 2 * index + 2)
                    job_done.wait(act, s, plan.order["diffuse2", NT - 1] + 1)
                elif name == "head_split":
                    head_written.wait(act, s, 2 * index + 2)
                    if plan.layer1:
                        used = ("hop12", NT - 1) if index < KT else ("diffuse1", NT - 1)
                        job_done.wait(act, s, plan.order[used] + 1)
                if name == "mixed_value":
                    b = bank[plan.bank[name, index]]
                    for half in range(2):
                        t = 2 * index + half
                        last = nc.scalar.activation(mixed_hi[:, t, :], b[:, half * D:(half + 1) * D], ACT.Identity,
                                                    scale=row_mask[:, t:t + 1])
                    last.then_inc(high_written.sem, 1)
                    return
                if name == "hop12":
                    nc.scalar.activation(hop1[:, index, :], bank[plan.bank[name, index]][:, 0:D], ACT.Copy)
                high, _ = parts(name, index)
                nc.scalar.activation(high, whole(plan, name, index), ACT.Copy).then_inc(high_written.sem, 1)

            plan_banks = {name for _, name, _ in FULL.jobs}

            def job(plan, s, name, index):
                if name in SPLITS:
                    split(plan, s, name, index)
                elif name == "adj_transpose":
                    b = bank[plan.bank[name, index]]
                    job_done.wait(act, s, plan.order[name, index] + 1)
                    nc.scalar.activation(adj_t[:, index, :], b[:, :], ACT.Copy)
                    if plan.layer1:
                        split_written.wait(act, s, plan.split["alpha_split", index] + 1)
                    if index == 3:
                        split_written.wait(act, s, plan.split["edge_split", 0] + 1)
                    nc.scalar.activation(edge_tile(0, index), b[:, :], ACT.Exp, scale=-1.0
                                         ).then_inc(edge_exp_written.sem, 1)
                elif name == "edge_score":
                    job_done.wait(act, s, plan.order["source_score", 0] + 1)
                    hop0_written.wait(act, s, NT)
                    if index == 0:
                        split_written.wait(act, s, 0)
                    nc.scalar.activation(edge_tile(1, index), bank[plan.bank["source_score", 0]][:, :], ACT.Identity,
                                         bias=target_score[:, index:index + 1]).then_inc(edge_score_written.sem, 1)
                elif name == "alpha_exp":
                    leaky_written.wait(act, s, index + 1)
                    nc.scalar.activation(edge_tile(1, index), edge_tile(1, index), ACT.Exp
                                         ).then_inc(alpha_exp_written.sem, 1)

            def exponent(s, u):
                i, half = u % NT, probs[:, u % BUFS, :]
                exp_bias_written.wait(act, s, u + 1)
                nc.scalar.activation(half, half, ACT.Exp, bias=exp_bias[:, u % 2:u % 2 + 1],
                                     scale=row_scale[:, i:i + 1], accum_out=row_sum[:, i:i + 1]
                                     ).then_inc(exp_written.sem, 1)

            def turned(ap_of, u):
                return ap_of[:, :, (u % NT) * P:(u % NT + 1) * P]

            def split_turned(s, u):
                probs_turned.wait(act, s, u + 1)
                half_done.wait(act, s, u // 2 - 1)
                nc.scalar.activation(turned(turned_hi, u), turned_bank[u % 2][:, :].rearrange("p (j i) -> p j i", j=NT),
                                     ACT.Copy).then_inc(turned_high.sem, 1)

            def take_head(s, h):
                rows = slice((h % 2) * DH, (h % 2 + 1) * DH)
                half_done.wait(act, s, 2 * h + 2)
                nc.scalar.activation(heads[rows, h // 2, :], out_bank[DH:2 * DH, :], ACT.Copy
                                     ).then_inc(head_low_copied.sem, 1)

            def step(s, plan):
                for slot in SLOTS:
                    if plan.layer0 and 0 <= slot - 3 < UNITS:
                        split_turned(s, slot - 3)
                    if plan.layer0 and slot % NT == 0 and 0 <= slot // NT - 2 < HEADS:
                        take_head(s, slot // NT - 2)
                    for name, index in plan.side[slot] + plan.taken[slot]:
                        job(plan, s, name, index)
                    if plan.layer0 and 0 <= slot < UNITS:
                        exponent(s, slot)

            step(-1, BEFORE)
            step(0, FIRST)
            with act.Fori(1, B - 1) as s:
                step(s, FULL)
            step(B - 1, FINAL)
            step(B, LAST)

        @block.vector
        def _(dve):
            setup = [0]

            def link(instruction):
                setup[0] += 1
                instruction.then_inc(setup_dve, 1)
                dve.wait_ge(setup_dve, setup[0])

            dve.wait_ge(mask_rows_loaded, 16)
            link(nc.vector.tensor_copy(mask_rows, mask_rows_u8))
            assert setup[0] == MASK_ROWS_STEP
            dve.wait_ge(small_loaded, 16 * 5)
            for t in range(KT):
                for o in range(2):
                    link(nc.vector.tensor_copy(att_pairs[:, t, o:o + 1], att_cols[:, o * KT + t, :]))
            dve.wait_ge(const_written, 1)
            for t in range(KT):
                link(nc.vector.tensor_scalar(bv_rep[:, t, :], ones, bv_cols[:, t, :], None, ALU.mult))
            dve.wait_ge(wout_loaded, 16)
            link(nc.vector.tensor_scalar(wout[:, :, :], wout[:, :, :], GAIN, None, ALU.mult))
            dve.wait_ge(setup_pe, 1)
            link(nc.vector.tensor_copy(mask_col[:, :], bank[0][:, 0:B * NT]))
            dve.wait_ge(setup_pe, 2)
            for t in range(HT):
                link(nc.vector.tensor_copy(wvh_t[:, t, :], bank[1 + t // 2][:, (t % 2) * D:(t % 2 + 1) * D]))
            dve.wait_ge(setup_pe, 3)
            link(nc.vector.tensor_copy(wv1_t, score_bank[0][:, :].rearrange("p (t d) -> p t d", t=KT)))
            assert setup[0] == PROJ_READY_STEP
            dve.wait_ge(setup_pe, 4)
            link(nc.vector.tensor_copy(wmix_raw, score_bank[1][:, :].rearrange("p (t d) -> p t d", t=KT)))
            dve.wait_ge(setup_pe, 5)
            link(nc.vector.tensor_copy(att_proj, turned_bank[0][:, 0:2 * KT].rearrange("p (t o) -> p t o", t=KT)))
            link(nc.vector.tensor_copy(bv_proj, turned_bank[1][:, 0:2]))
            link(nc.vector.tensor_tensor(score_const[:, :], bv_proj[:, 0:1], bv_proj[:, 1:2], ALU.add))
            link(nc.vector.tensor_tensor(score_const[:, :], score_const[:, :], att_b_all, ALU.add))
            for t in range(KT):
                link(nc.vector.tensor_scalar(src_rep[:, t, :], ones, att_proj[:, t, 1:2], None, ALU.mult))
            assert setup[0] == ATT_PROJ_STEP
            hi = 0
            for t in range(KT):
                cols = wqkv_raw[t].rearrange("p (h i d) -> p i h d", h=HEADS, i=3)
                for i in range(3):
                    hi += 1
                    dve.wait_ge(setup_hi, hi)
                    link(nc.vector.tensor_tensor(
                        wqkv_lo[:, t, i, :].rearrange("p (h d) -> p h d", h=HEADS), cols[:, i],
                        f32(wqkv_hi[:, t, i, :]).rearrange("p (h d) -> p h d", h=HEADS), ALU.subtract))
            for t in range(KT):
                hi += 1
                dve.wait_ge(setup_hi, hi)
                link(nc.vector.tensor_tensor(w12_lo[:, t, :].rearrange("p (k d) -> p k d", k=2), wk_raw[:, t, 1:3, :],
                                             f32(w12_hi[:, t, :]).rearrange("p (k d) -> p k d", k=2), ALU.subtract))
            for t in range(KT):
                for lo, raw, high in ((w0_lo[:, t, 0:D], wk_raw[:, t, 0, :], w0_hi[:, t, 0:D]),
                                      (w0_lo[:, t, D:D + 2], att_proj[:, t, :], w0_hi[:, t, D:D + 2]),
                                      (wsrc_lo[:, t, :], src_rep[:, t, :], wsrc_hi[:, t, :]),
                                      (wmix_lo[:, t, :], wmix_raw[:, t, :], wmix_hi[:, t, :])):
                    hi += 1
                    dve.wait_ge(setup_hi, hi)
                    link(nc.vector.tensor_tensor(lo, raw, f32(high), ALU.subtract))
            for t in range(HT):
                hi += 1
                dve.wait_ge(setup_hi, hi)
                link(nc.vector.tensor_tensor(wout_lo[:, t, :], wout[:, t, :], f32(wout_hi[:, t, :]), ALU.subtract))
            link(nc.vector.tensor_tensor(bk_sum[:, :], bk_raw[:, 0, :], bk_raw[:, 1, :], ALU.add))
            link(nc.vector.tensor_tensor(bk_sum[:, :], bk_sum[:, :], bk_raw[:, 2, :], ALU.add))
            link(nc.vector.tensor_copy(hop_hi[:, :, D:D + 2], ones_pairs))
            link(nc.vector.tensor_scalar(hop_lo[:, :, D:D + 2], ones_pairs, 0.0, None, ALU.mult))
            link(nc.vector.memset(neg_half[:, :], -0.5))
            assert setup[0] == SETUP_DVE_STEPS, setup[0]

            def masks(s):
                exp_written.wait(dve, s, 0)
                col = mask_col[:, bass.ds(s * NT, NT)]
                nc.vector.tensor_copy(row_mask[:, :], col)
                nc.vector.tensor_scalar(row_scale[:, :], col, SCORE_SCALE, None, ALU.mult)
                nc.vector.tensor_scalar(row_neg_scale[:, :], col, -SCORE_SCALE, None, ALU.mult
                                        ).then_inc(row_masks_written.sem, 1)
                mask_loaded.wait(dve, s, 1, 16)
                nc.vector.tensor_scalar(column_bias[:, :], mask_in[:, :], -1.0, MASKED, ALU.add, ALU.mult
                                        ).then_inc(mask_read.sem, 1)
                mask_read.wait(dve, s, 1)
                row_masks_written.wait(dve, s, 1)

            def score_max(s, u):
                i = u % NT
                scores_done.wait(dve, s, u + 1)
                probs_turned.wait(dve, s, u - 1 if u < 2 else u - 2)
                nc.vector.memset(wait_carrier[:, :], 0.0)
                nc.vector.tensor_tensor_reduce(
                    out=probs[:, u % BUFS, :], in0=score_bank[u % 2][:, :], in1=column_bias[:, :], scale=1.0,
                    scalar=LOWEST, op0=ALU.add, op1=ALU.max, accum_out=row_max[:, u % 2:u % 2 + 1]
                ).then_inc(max_written.sem, 1)
                max_written.wait(dve, s, u + 1)
                nc.vector.tensor_tensor(exp_bias[:, u % 2:u % 2 + 1], row_max[:, u % 2:u % 2 + 1],
                                        row_neg_scale[:, i:i + 1], ALU.mult).then_inc(exp_bias_written.sem, 1)

            def invert_sum(s, u):
                i = u % NT
                exp_written.wait(dve, s, u + 1)
                nc.vector.reciprocal(row_inv[:, i:i + 1], row_sum[:, i:i + 1]).then_inc(inv_written.sem, 1)

            def split_turned(s, u):
                cols = slice((u % NT) * P, (u % NT + 1) * P)
                turned_high.wait(dve, s, u + 1)
                nc.vector.tensor_tensor(turned_lo[:, :, cols], turned_bank[u % 2][:, :].rearrange("p (j i) -> p j i", j=NT),
                                        f32(turned_hi[:, :, cols]), ALU.subtract).then_inc(turned_split.sem, 1)

            def take_head(s, h):
                rows = slice((h % 2) * DH, (h % 2 + 1) * DH)
                head_low_copied.wait(dve, s, h + 1)
                nc.vector.tensor_tensor(heads[rows, h // 2, :], out_bank[0:DH, :], heads[rows, h // 2, :], ALU.add
                                        ).then_inc(head_written.sem, 1)

            def moments(s, src, written, stats, mean, var, signal):
                for t in range(NT):
                    written(t)
                    nc.vector.bn_stats(stats[:, t, :], src[:, t, :]).then_inc(signal.sem, 1)
                signal.wait(dve, s, NT)
                nc.vector.memset(wait_carrier[:, :], 0.0)
                for t in range(NT):
                    nc.vector.bn_aggr(mean[:, t, :], stats[:, t, :]).then_inc(signal.sem, 1)
                signal.wait(dve, s, 2 * NT)
                nc.vector.tensor_scalar(var[:, :], mean[:, :, 1], EPS_NORM, None, ALU.add).then_inc(signal.sem, 1)

            def split(plan, s, name, index):
                high_written.wait(dve, s, plan.split[name, index] + 1)
                if name == "mixed_value":
                    b = bank[plan.bank[name, index]]
                    for half in range(2):
                        t = 2 * index + half
                        last = nc.vector.scalar_tensor_tensor(
                            out=mixed_lo[:, t, :], in0=b[:, half * D:(half + 1) * D], scalar=row_mask[:, t:t + 1],
                            in1=f32(mixed_hi[:, t, :]), op0=ALU.mult, op1=ALU.subtract)
                    last.then_inc(split_written.sem, 1)
                    return
                high, low = parts(name, index)
                nc.vector.tensor_tensor(low, whole(plan, name, index), f32(high), ALU.subtract
                                        ).then_inc(split_written.sem, 1)

            def normalize(s, src, dst, mean, rstd, written):
                for t in range(NT):
                    nc.vector.tensor_scalar(dst[:, t, :], src[:, t, :], mean[:, t, 0:1], rstd[:, t:t + 1],
                                            ALU.subtract, ALU.mult).then_inc(written, 1)

            def job(plan, s, name, index):
                if name in SPLITS:
                    split(plan, s, name, index)
                elif name == "moments0":
                    moments(s, mix, lambda t: mix_written.wait(dve, s, 0), stats0, mean0, var0, moments0)
                elif name == "normalize0":
                    rstd0_written.wait(dve, s, 1)
                    normalize(s, mix, x1, mean0, rstd0, x1_written.sem)
                elif name == "moments1":
                    moments(s, y, lambda t: y_written.wait(dve, s, t + 1), stats1, mean1, var1, moments1)
                elif name == "normalize1":
                    rstd1_written.wait(dve, s, 1)
                    for t in range(NT):
                        last = nc.vector.tensor_scalar(y[:, t, :], y[:, t, :], mean1[:, t, 0:1],
                                                       rstd1[:, t:t + 1], ALU.subtract, ALU.mult)
                    last.then_inc(out_written.sem, 1)
                elif name == "edge_score":
                    half = edge_tile(1, index)
                    edge_score_written.wait(dve, s, index + 1)
                    nc.vector.scalar_tensor_tensor(out=half, in0=half, scalar=SLOPE, in1=half,
                                                   op0=ALU.mult, op1=ALU.max).then_inc(leaky_written.sem, 1)
                elif name == "adj_product":
                    job_done.wait(dve, s, plan.order[name, index] + 1)
                    x_bias_written.wait(dve, s, 1)
                    nc.vector.scalar_tensor_tensor(
                        out=mix[:, index, :], in0=bank[plan.bank[name, index]][:, 0:D],
                        scalar=row_mask[:, index:index + 1], in1=mix[:, index, :], op0=ALU.mult, op1=ALU.add
                    ).then_inc(adj_part_written.sem, 1)
                elif name == "out_product":
                    rows = slice(2 * index, 2 * index + 2)
                    job_done.wait(dve, s, plan.order[name, index] + 1)
                    adj_part_written.wait(dve, s, 2 * index + 2)
                    nc.vector.tensor_tensor(mix[:, rows, :], halves(bank[plan.bank[name, index]]), mix[:, rows, :],
                                            ALU.add).then_inc(mix_written.sem, 1)
                elif name == "hop0":
                    b = bank[plan.bank[name, index]]
                    if index == 0:
                        out_stored.wait(dve, s, 0, 16)
                    job_done.wait(dve, s, plan.order[name, index] + 1)
                    nc.vector.tensor_tensor(y[:, index, :], b[:, 0:D], bk_sum[:, :], ALU.add)
                    nc.vector.tensor_tensor(target_score[:, index:index + 1], b[:, D:D + 1], score_const[:, :],
                                            ALU.add).then_inc(hop0_written.sem, 1)
                elif name == "diffuse2":
                    b = bank[plan.bank[name, index]]
                    job_done.wait(dve, s, plan.order[name, index] + 1)
                    nc.vector.tensor_scalar(alpha_sum[:, index:index + 1], b[:, D:D + 1], EPS_SUM, None, ALU.add
                                            ).then_inc(alpha_sum_written.sem, 1)
                    alpha_sum_written.wait(dve, s, index + 1)
                    nc.vector.reciprocal(alpha_inv[:, index:index + 1], alpha_sum[:, index:index + 1]
                                         ).then_inc(alpha_inv_written.sem, 1)
                    alpha_inv_written.wait(dve, s, index + 1)
                    nc.vector.scalar_tensor_tensor(
                        out=hop1[:, index, :], in0=b[:, 0:D], scalar=alpha_inv[:, index:index + 1],
                        in1=hop1[:, index, :], op0=ALU.mult, op1=ALU.add).then_inc(hop1_written.sem, 1)
                elif name == "diffuse1":
                    job_done.wait(dve, s, plan.order[name, index] + 1)
                    nc.vector.scalar_tensor_tensor(
                        out=y[:, index, :], in0=bank[plan.bank[name, index]][:, 0:D],
                        scalar=alpha_inv[:, index:index + 1], in1=y[:, index, :], op0=ALU.mult, op1=ALU.add
                    ).then_inc(hops_summed.sem, 1)
                    hops_summed.wait(dve, s, index + 1)
                    nc.vector.scalar_tensor_tensor(out=y[:, index, :], in0=y[:, index, :], scalar=0.0,
                                                   in1=x1[:, index, :], op0=ALU.max, op1=ALU.add
                                                   ).then_inc(y_written.sem, 1)

            def step(s, plan):
                if plan.layer0:
                    masks(s)
                for slot in SLOTS:
                    if plan.layer0 and 0 <= slot < UNITS:
                        score_max(s, slot)
                    if plan.layer0 and 0 <= slot - 1 < UNITS:
                        invert_sum(s, slot - 1)
                    if plan.layer0 and 0 <= slot - 3 < UNITS:
                        split_turned(s, slot - 3)
                    if plan.layer0 and slot % NT == 0 and 0 <= slot // NT - 2 < HEADS:
                        take_head(s, slot // NT - 2)
                    for name, index in plan.side[slot] + plan.taken[slot]:
                        job(plan, s, name, index)

            step(-1, BEFORE)
            step(0, FIRST)
            with dve.Fori(1, B - 1) as s:
                step(s, FULL)
            step(B - 1, FINAL)
            step(B, LAST)

        @block.gpsimd
        def _(pool):
            nc.gpsimd.memset(ones, 1.0).then_inc(const_written, 1)
            pool.wait_ge(const_written, 1)
            nc.gpsimd.affine_select(out=ident[:, :], in_=ones, compare_op=ALU.is_equal, fill=0.0, base=0,
                                    pattern=[[-1, P]], channel_multiplier=1).then_inc(ident_written, 1)
            pool.wait_ge(small_loaded, 16 * 5)
            pool.wait_ge(setup_dve, SETUP_DVE_STEPS)

            def reciprocal_root(s, moments, rstd, var, signal):
                moments.wait(pool, s, 2 * NT + 1)
                nc.gpsimd.tensor_tensor(rstd[:, :], var[:, :], neg_half[:, :], ALU.pow).then_inc(signal.sem, 1)

            def normalize(s, u):
                i = u % NT
                inv_written.wait(pool, s, u + 1)
                nc.gpsimd.tensor_tensor(probs[:, u % BUFS, :], probs[:, u % BUFS, :],
                                        row_inv[:, i:i + 1].broadcast_to([P, N]), ALU.mult
                                        ).then_inc(probs_written.sem, 1)

            def add_bias(s, plan, t):
                if t == 0:
                    x_loaded.wait(pool, s, 1, 16)
                    if plan.layer1:
                        x1_written.wait(pool, s, NT)
                last = nc.gpsimd.tensor_tensor(mix[:, t, :], x_in[:, t, :], b_out_all[:, :], ALU.add)
                if t == NT - 1:
                    last.then_inc(x_bias_written.sem, 1)

            def step(s, plan):
                for slot in SLOTS:
                    if plan.layer0 and 0 <= slot - 1 < UNITS:
                        normalize(s, slot - 1)
                    if plan.layer0 and 5 <= slot < 5 + NT:
                        add_bias(s, plan, slot - 5)
                    for name, index in plan.side[slot] + plan.taken[slot]:
                        half = edge_tile(0 if name == "adj_transpose" else 1, index)
                        if name == "moments0":
                            reciprocal_root(s, moments0, rstd0, var0, rstd0_written)
                        elif name == "moments1":
                            reciprocal_root(s, moments1, rstd1, var1, rstd1_written)
                        elif name == "alpha_exp":
                            alpha_exp_written.wait(pool, s, index + 1)
                            nc.gpsimd.tensor_tensor(half, half, adj_t[:, index, :], ALU.mult
                                                    ).then_inc(alpha_written.sem, 1)
                        elif name == "adj_transpose":
                            edge_exp_written.wait(pool, s, index + 1)
                            nc.gpsimd.tensor_tensor(half, half, adj_t[:, index, :], ALU.add
                                                    ).then_inc(edge_written.sem, 1)

            step(-1, BEFORE)
            step(0, FIRST)
            with pool.Fori(1, B - 1) as s:
                step(s, FULL)
            step(B - 1, FINAL)
            step(B, LAST)


MASK_ROWS_STEP = 1
PROJ_READY_STEP = MASK_ROWS_STEP + 4 + 2 + 1 + 1 + 4 + 1
ATT_PROJ_STEP = PROJ_READY_STEP + 1 + 2 + 2 + 2
SETUP_DVE_STEPS = ATT_PROJ_STEP + 6 + 2 + 8 + 4 + 2 + 3

_INS = ['x', 'adj', 'nodemask', 'L0_gnn_W_qkv', 'L0_gnn_W_out', 'L0_gnn_b_out', 'L1_gnn_Wv', 'L1_gnn_bv',
        'L1_gnn_aw', 'L1_gnn_ab', 'L1_gnn_Wk', 'L1_gnn_bk']


def kernel(**inputs):
    import numpy as _np
    import concourse.bacc as _bacc
    from concourse import mybir as _mybir
    from concourse.bass_utils import run_bass_kernel_spmd as _run

    nc = _bacc.Bacc("TRN2", target_bir_lowering=False, num_devices=1)
    arrays, args = {}, []
    for name in _INS:
        a = _np.ascontiguousarray(inputs[name])
        arrays[f"in_{name}_dram"] = a
        args.append(nc.dram_tensor(f"in_{name}_dram", a.shape, _mybir.dt.from_np(a.dtype), kind="ExternalInput").ap())
    shape = inputs["x"].shape
    args.append(nc.dram_tensor("out_0_dram", shape, _mybir.dt.float32, kind="ExternalOutput").ap())
    graph_layers(nc, *args)
    r = _run(nc, [arrays], core_ids=[0])
    return r.results[0]["out_0_dram"]
```

```python
from contextlib import ExitStack

import concourse.bass as bass
from concourse import mybir

P = 128
F32 = mybir.dt.float32
F32R = mybir.dt.float32r
BF16 = mybir.dt.bfloat16
U8 = mybir.dt.uint8
ALU = mybir.AluOpType
ACT = mybir.ActivationFunctionType

HEADS = 8
DH = 64
GAIN = 0.33
SCORE_SCALE = DH ** -0.5
SLOPE = 0.2
EPS_NORM = 1e-5
EPS_SUM = 1e-12
MASKED = 1e30
LOWEST = -3.0e38

LAYER0_JOBS = [
    (0, "value", 0), (1, "value", 1), (2, "value", 2), (3, "value", 3),
    (1.5, "query", 1), (4, "key", 1), (8, "query", 2), (10, "key", 2), (17.5, "query", 3), (19.5, "key", 3),
    (9, "mixed_value", 0), (12, "mixed_value", 1),
    (21.5, "adj_transpose", 0), (26, "adj_transpose", 1), (29.7, "adj_transpose", 2), (30, "adj_transpose", 3)]
LAYER1_JOBS = [
    (4, "adj_product", 0), (5, "adj_product", 1), (5, "adj_product", 2), (6, "adj_product", 3),
    (6, "out_product", 0), (7, "out_product", 1),
    (11, "x1_transpose", 0), (11, "x1_transpose", 1),
    (13, "hop0", 0), (13, "hop0", 1), (14, "hop0", 2), (15, "hop0", 3), (15.5, "source_score", 0),
    (16, "hop12", 0), (17, "hop12", 1), (18, "hop12", 2), (19, "hop12", 3),
    (22, "diffuse2", 0), (23, "diffuse2", 1), (24, "diffuse2", 2), (24.5, "diffuse2", 3),
    (26.5, "diffuse1", 0), (27, "diffuse1", 1), (28, "diffuse1", 2), (28.5, "diffuse1", 3)]
NEXT_JOBS = [(20.5, "x_transpose", 0), (22.5, "x_transpose", 1), (25, "query", 0), (29.5, "key", 0)]
LAYER0_SIDE = [(10, "keep_mask", 0), (17, "keep_value", 0), (20, "head_split", 0), (22, "head_split", 1)]
LAYER1_SIDE = [(0, "edge_split", 0), (1, "edge_split", 1), (1, "head_split", 2), (1, "edge_split", 2),
               (2, "edge_split", 3), (4, "head_split", 3), (7, "stats0", 0), (8, "stats0", 1),
               (8, "moments0", 0), (10, "normalize0", 0),
               (16, "edge_score", 0), (16, "edge_score", 1), (16, "edge_score", 2), (16, "edge_score", 3),
               (16, "leaky", 0), (16, "leaky", 1), (17, "leaky", 2), (17, "leaky", 3),
               (17, "alpha_exp", 0), (17, "alpha_exp", 1), (18, "alpha_exp", 2), (18, "alpha_exp", 3),
               (19, "alpha_split", 0), (19, "alpha_split", 1), (20, "alpha_split", 2), (20, "alpha_split", 3),
               (25, "hop1_split", 0), (25, "hop1_split", 1), (30, "moments1", 0), (31, "normalize1", 0)]
SPLITS = ("x_transpose", "query", "key", "value", "mixed_value", "x1_transpose", "hop12",
          "head_split", "hop1_split")
RING = 3
X_BIAS_SLOT = 10
SLOTS = range(32)


class Plan:

    def __init__(self, layer0, layer1, following, offset):
        jobs = (LAYER0_JOBS if layer0 else []) + (LAYER1_JOBS if layer1 else []) + (NEXT_JOBS if following else [])
        side = (LAYER0_SIDE if layer0 else []) + (LAYER1_SIDE if layer1 else [])
        self.jobs = sorted(jobs, key=lambda j: j[0])
        self.layer0, self.layer1 = layer0, layer1
        self.slots = {slot: [j[1:] for j in self.jobs if int(j[0]) == slot] for slot in SLOTS}
        self.side = {slot: [j[1:] for j in side if j[0] == slot] for slot in SLOTS}
        self.order = {j[1:]: n for n, j in enumerate(self.jobs)}
        self.bank = {j[1:]: (n + offset) % RING for n, j in enumerate(self.jobs)}
        self.taken = {slot: [] for slot in SLOTS}
        for slot, *j in self.jobs:
            self.taken[int(slot) + 1].append(tuple(j))
        split = [j for slot in SLOTS for j in self.taken[slot] + self.side[slot] if j[0] in SPLITS]
        self.split = {j: n for n, j in enumerate(split)}

    def unit(self, slot, lag):
        if slot >= lag:
            return (0, slot - lag) if self.layer0 else None
        return (1, slot - lag + len(SLOTS)) if self.layer1 else None


FULL = Plan(True, True, True, 0)
assert len(FULL.jobs) % RING == 0
FIRST = Plan(True, False, True, -len(LAYER0_JOBS + NEXT_JOBS))
BEFORE = Plan(False, False, True, -len(LAYER0_JOBS + 2 * NEXT_JOBS))
FINAL = Plan(True, True, False, 0)
LAST = Plan(False, True, False, len(FINAL.jobs))
BEFORE.previous, FIRST.previous, FULL.previous, FINAL.previous, LAST.previous = None, BEFORE, FULL, FULL, FINAL
assert [j[1:] for j in FIRST.jobs[-RING:]] == [j[1:] for j in FULL.jobs[-RING:]]
assert [len(FIRST.split) - FIRST.split.get(j[1:], 0) for j in FIRST.jobs[-RING:] if j[1] in SPLITS] == \
       [len(FULL.split) - FULL.split.get(j[1:], 0) for j in FULL.jobs[-RING:] if j[1] in SPLITS]


class Signal:

    def __init__(self, sem, before, first, full, last, final):
        self.sem, self.before, self.first, self.full, self.last, self.final = sem, before, first, full, last, final

    def total(self, step, count, unit=1):
        if isinstance(step, int):
            start = 0 if step < 0 else self.before
            start += self.first if step > 0 else 0
            start += (min(step, self.final) - 1) * self.full if step > 1 else 0
            start += self.last if step > self.final else 0
            return (start + count) * unit
        return step * (self.full * unit) + (self.before + self.first - self.full + count) * unit

    def wait(self, eng, step, count, unit=1, back=0):
        value = self.total(step - back, count, unit)
        if isinstance(value, int):
            if value > 0:
                eng.wait_ge(self.sem, value)
            return
        assert self.total(1 - back, count) > 0, "a wait on a register must be on a value above zero"
        eng.wait_ge(self.sem, value)


def graph_layers(nc, x, adj, nodemask, w_qkv, w_out, b_out, w_v, b_v, att_w, att_b, w_k, b_k, out):
    B, N, D = x.shape
    NT = N // P
    KT = D // P
    HD = HEADS * DH
    HT = HD // P
    UNITS = HEADS * NT
    HOPS = w_k.shape[0]
    BUFS = 4
    assert UNITS == len(SLOTS) and UNITS % BUFS == 0 and NT == 4 and KT == 2 and HT == 4 and HOPS == 3 and N == 512

    ctx = ExitStack()
    with ctx:
        def sb(name, shape, dt=F32):
            return ctx.enter_context(nc.sbuf_tensor(name, shape, dt))

        def sem(name):
            return ctx.enter_context(nc.semaphore(name))

        def every(name, count):
            return Signal(sem(name), 0, count, count, count, B - 1)

        def layer1_only(name, count):
            return Signal(sem(name), 0, 0, count, count, B - 1)

        def planned(name, count):
            return Signal(sem(name), count(BEFORE), count(FIRST), count(FULL), count(FINAL), B - 1)

        x_in = sb("x_in", [P, NT, D])
        adj_in = sb("adj_in", [P, NT, N // 2])
        mask_in = sb("mask_in", [P, N], U8)
        mix = sb("mix", [P, NT, D])
        x_hi, x_lo = sb("x_hi", [P, KT, N], F32R), sb("x_lo", [P, KT, N], F32R)
        q_hi, q_lo = sb("q_hi", [P, 2, N], F32R), sb("q_lo", [P, 2, N], F32R)
        k_hi, k_lo = sb("k_hi", [P, 2, N], F32R), sb("k_lo", [P, 2, N], F32R)
        value = sb("value", [P, NT, HEADS, 2, DH], F32R)
        last_value = sb("last_value", [P, NT, 2, DH], F32R)
        mixed_hi, mixed_lo = sb("mixed_hi", [P, NT, D], F32R), sb("mixed_lo", [P, NT, D], F32R)
        column_bias = sb("column_bias", [P, N], BF16)
        row_mask = sb("row_mask", [P, NT])
        closing_mask = sb("closing_mask", [P, NT])
        row_scale = sb("row_scale", [P, NT])
        row_neg_scale = sb("row_neg_scale", [P, NT])
        row_max = sb("row_max", [P, 2])
        exp_bias = sb("exp_bias", [P, 2])
        row_sum = sb("row_sum", [P, NT])
        row_inv = sb("row_inv", [P, NT])
        probs = sb("probs", [P, BUFS, N])
        turned_hi, turned_lo = sb("turned_hi", [P, NT, N], F32R), sb("turned_lo", [P, NT, N], F32R)
        heads = sb("heads", [P, 2, N])
        adj_t = sb("adj_t", [P, NT, N])
        edge_hi, edge_lo = sb("edge_hi", [P, NT, N], F32R), sb("edge_lo", [P, NT, N], F32R)
        edge = sb("edge", [P, NT, N])
        x1 = sb("x1", [P, NT, D])
        x1_hi, x1_lo = sb("x1_hi", [P, KT, N], F32R), sb("x1_lo", [P, KT, N], F32R)
        y = sb("y", [P, NT, D])
        hop1 = sb("hop1", [P, NT, D])
        hop_hi, hop_lo = sb("hop_hi", [P, NT, D + 2], F32R), sb("hop_lo", [P, NT, D + 2], F32R)
        target_score = sb("target_score", [P, NT])
        alpha_inv = sb("alpha_inv", [P, NT])
        alpha_sum = sb("alpha_sum", [P, NT])
        stats0, stats1 = sb("stats0", [P, NT, 6]), sb("stats1", [P, NT, 6])
        mean0, mean1 = sb("mean0", [P, NT, 2]), sb("mean1", [P, NT, 2])
        var0, var1 = sb("var0", [P, NT]), sb("var1", [P, NT])
        rstd0, rstd1 = sb("rstd0", [P, NT]), sb("rstd1", [P, NT])
        neg_mean0, neg_mean1 = sb("neg_mean0", [P, NT]), sb("neg_mean1", [P, NT])
        shift0, shift1 = sb("shift0", [P, NT]), sb("shift1", [P, NT])
        wait_carrier = sb("wait_carrier", [P, 1])

        ident = sb("ident", [P, P])
        neg_half = sb("neg_half", [P, NT])
        mask_col = sb("mask_col", [P, B * NT])
        wqkv_hi = sb("wqkv_hi", [P, KT, 3, HD], F32R)
        wqkv_lo = sb("wqkv_lo", [P, KT, 3, HD], F32R)
        wout_hi, wout_lo = sb("wout_hi", [P, HT, D], F32R), sb("wout_lo", [P, HT, D], F32R)
        wmix_hi, wmix_lo = sb("wmix_hi", [P, KT, D], F32R), sb("wmix_lo", [P, KT, D], F32R)
        w12_hi, w12_lo = sb("w12_hi", [P, KT, 2 * D], F32R), sb("w12_lo", [P, KT, 2 * D], F32R)
        w0_hi, w0_lo = sb("w0_hi", [P, KT, D + 2], F32R), sb("w0_lo", [P, KT, D + 2], F32R)
        wsrc_hi, wsrc_lo = sb("wsrc_hi", [P, KT, P], F32R), sb("wsrc_lo", [P, KT, P], F32R)
        b_out_all = sb("b_out_all", [P, D])
        bk_sum = sb("bk_sum", [P, D])
        score_const = sb("score_const", [P, 1])

        def flat(t):
            return t[:, :, :].rearrange("p a b -> p (a b)")

        wqkv_raw = [flat(adj_t)[:, 0:3 * HD], flat(probs)[:, 0:3 * HD]]
        wk_raw = flat(edge)[:, 0:KT * HOPS * D].rearrange("p (t k d) -> p t k d", t=KT, k=HOPS)
        ones = flat(edge)[:, KT * HOPS * D:KT * HOPS * D + P]
        ones_pairs = ones[:, 0:2 * NT].rearrange("p (t o) -> p t o", t=NT)
        wout = mix
        wv_raw = hop1[:, 0:KT, :]
        wv1_t = hop1[:, KT:2 * KT, :]
        wvh = flat(x1).rearrange("p (t n) -> p t n", t=KT)
        wvh_t = y
        wmix_raw = flat(adj_t)[:, 3 * HD:3 * HD + KT * D].rearrange("p (t d) -> p t d", t=KT)
        bv_rep = flat(heads)[:, HOPS * D:HOPS * D + KT * P].rearrange("p (t m) -> p t m", t=KT)
        src_rep = flat(edge)[:, KT * HOPS * D + P:KT * HOPS * D + P + KT * P].rearrange("p (t m) -> p t m", t=KT)
        bk_raw = flat(heads)[:, 0:HOPS * D].rearrange("p (k d) -> p k d", k=HOPS)
        small = probs[:, 3, :]
        att_cols = small[:, 0:4].rearrange("p (g o) -> p g o", o=1)
        bv_cols = small[:, 4:6].rearrange("p (g o) -> p g o", o=1)
        att_pairs = small[:, 6:10].rearrange("p (t o) -> p t o", t=KT)
        att_b_all = small[:, 10:11]
        att_proj = small[:, 12:16].rearrange("p (t o) -> p t o", t=KT)
        bv_proj = small[:, 16:18]
        mask_rows = small[0:B * NT, P:2 * P]
        mask_rows_u8 = mask_in[0:B * NT, 0:P]

        bank = [ctx.enter_context(nc.psum_tensor(f"job_bank{i}", [P, 512], F32)) for i in range(RING)]
        score_bank = [ctx.enter_context(nc.psum_tensor(f"score_bank{i}", [P, 512], F32)) for i in range(2)]
        turned_bank = [ctx.enter_context(nc.psum_tensor(f"turned_bank{i}", [P, 512], F32)) for i in range(2)]
        out_bank = ctx.enter_context(nc.psum_tensor("out_bank", [P, 512], F32))

        def parts(name, index):
            slot = index % 2
            rows2 = slice(2 * index, 2 * index + 2)
            return {
                "x_transpose": lambda: (x_hi[:, slot, :], x_lo[:, slot, :]),
                "x1_transpose": lambda: (x1_hi[:, slot, :], x1_lo[:, slot, :]),
                "query": lambda: (q_hi[:, slot, :], q_lo[:, slot, :]),
                "key": lambda: (k_hi[:, slot, :], k_lo[:, slot, :]),
                "value": lambda: (value[:, index, :, 0, :], value[:, index, :, 1, :]),
                "hop12": lambda: (hop_hi[:, index, 0:D], hop_lo[:, index, 0:D]),
                "hop1_split": lambda: (hop_hi[:, rows2, 0:D], hop_lo[:, rows2, 0:D]),
                "head_split": lambda: (x1_hi[:, slot, :], x1_lo[:, slot, :]) if index < KT else
                                      (hop_hi[:, 2 * slot:2 * slot + 2, 0:D], hop_lo[:, 2 * slot:2 * slot + 2, 0:D]),
            }[name]()

        def head_rows(t, i):
            if t < KT:
                return x1_hi[:, t, i * P:(i + 1) * P], x1_lo[:, t, i * P:(i + 1) * P]
            cols = slice((i % 2) * P, (i % 2 + 1) * P)
            return tuple(part[:, 2 * (t - KT) + i // 2, cols] for part in (hop_hi, hop_lo))

        def whole(plan, name, index):
            if name == "hop1_split":
                return hop1[:, 2 * index:2 * index + 2, :]
            if name == "head_split":
                tile = heads[:, index % 2, :]
                return tile if index < KT else tile.rearrange("p (a d) -> p a d", a=2)
            b = bank[plan.bank[name, index]]
            if name == "hop12":
                return b[:, D:2 * D]
            if name == "value":
                return b[:, :].rearrange("p (h d) -> p h d", h=HEADS)
            return b[:, :]

        x_loaded = every("x_loaded", 1)
        adj_loaded = every("adj_loaded", 2)
        mask_loaded = every("mask_loaded", 1)
        mask_read = every("mask_read", 1)
        row_masks_written = every("row_masks_written", 1)
        x_bias_written = every("x_bias_written", 1)
        job_done = planned("job_done", lambda plan: len(plan.jobs))
        high_written = planned("high_written", lambda plan: len(plan.split))
        split_written = planned("split_written", lambda plan: len(plan.split))
        scores_done = every("scores_done", UNITS)
        max_written = every("max_written", UNITS)
        exp_bias_written = every("exp_bias_written", UNITS)
        exp_written = every("exp_written", UNITS)
        inv_written = every("inv_written", UNITS)
        probs_written = every("probs_written", UNITS)
        probs_turned = every("probs_turned", UNITS)
        turned_high = every("turned_high", UNITS)
        turned_split = every("turned_split", UNITS)
        half_done = every("half_done", 2 * HEADS)
        head_low_copied = every("head_low_copied", HEADS)
        head_written = every("head_written", HEADS)
        edge_exp_written = every("edge_exp_written", NT)
        edge_written = every("edge_written", NT)
        adj_part_written = every("adj_part_written", NT)
        mix_written = every("mix_written", 2)
        moments0 = layer1_only("moments0", 2 * NT + 1)
        rstd0_written = layer1_only("rstd0_written", 1)
        shift0_written = layer1_only("shift0_written", 1)
        edge_high = layer1_only("edge_high", 2 * NT)
        edge_split = layer1_only("edge_split", 2 * NT)
        value_kept = every("value_kept", 1)
        mask_kept = every("mask_kept", 1)
        x1_written = layer1_only("x1_written", NT)
        hop0_written = layer1_only("hop0_written", NT)
        edge_score_written = layer1_only("edge_score_written", NT)
        leaky_written = layer1_only("leaky_written", NT)
        alpha_exp_written = layer1_only("alpha_exp_written", NT)
        alpha_written = layer1_only("alpha_written", NT)
        alpha_sum_written = layer1_only("alpha_sum_written", NT)
        alpha_inv_written = layer1_only("alpha_inv_written", NT)
        hop1_written = layer1_only("hop1_written", NT)
        hops_summed = layer1_only("hops_summed", NT)
        y_written = layer1_only("y_written", NT)
        moments1 = layer1_only("moments1", 2 * NT + 1)
        rstd1_written = layer1_only("rstd1_written", 1)
        shift1_written = layer1_only("shift1_written", 1)
        out_written = layer1_only("out_written", 1)
        out_stored = every("out_stored", 1)

        wqkv_loaded = sem("wqkv_loaded")
        wk_loaded = sem("wk_loaded")
        small_loaded = sem("small_loaded")
        wout_loaded = sem("wout_loaded")
        wv_loaded = sem("wv_loaded")
        mask_rows_loaded = sem("mask_rows_loaded")
        const_written = sem("const_written")
        ident_written = sem("ident_written")
        setup_act = sem("setup_act")
        setup_dve = sem("setup_dve")
        setup_pe = sem("setup_pe")
        setup_hi = sem("setup_hi")

        def f32(t):
            return t.bitcast(F32)

        def halves(b):
            return b[:, :].rearrange("p (a d) -> p a d", a=2)

        block = ctx.enter_context(nc.Block())

        @block.sync
        def _(sp):
            for t in range(KT):
                sp.dma_start(wqkv_raw[t], w_qkv[t * P:(t + 1) * P, :]).then_inc(wqkv_loaded, 16)
            sp.dma_start(wout[:, :, :], w_out.rearrange("(t p) d -> p t d", p=P)).then_inc(wout_loaded, 16)
            sp.dma_start(wv_raw, w_v.rearrange("(t p) d -> p t d", p=P)).then_inc(wv_loaded, 16)
            for t in range(KT):
                sp.dma_start(wk_raw[:, t, :, :], w_k[:, t * P:(t + 1) * P, :].rearrange("k p d -> p k d")
                             ).then_inc(wk_loaded, 16)
            sp.dma_start(att_cols, att_w.rearrange("(g p) o -> p g o", p=P), allow_slow_non_contiguous=True
                         ).then_inc(small_loaded, 16)
            sp.dma_start(bv_cols, b_v.rearrange("(g p o) -> p g o", p=P, o=1), allow_slow_non_contiguous=True
                         ).then_inc(small_loaded, 16)
            sp.dma_start(att_b_all, att_b.rearrange("(a o) -> a o", a=1).broadcast_to([P, 1])
                         ).then_inc(small_loaded, 16)
            sp.dma_start(b_out_all[:, :], b_out.rearrange("(a d) -> a d", a=1).broadcast_to([P, D])
                         ).then_inc(small_loaded, 16)
            sp.dma_start(bk_raw, b_k.rearrange("(a k) d -> a k d", a=1).broadcast_to([P, HOPS, D])
                         ).then_inc(small_loaded, 16)
            sp.dma_start(mask_rows_u8, nodemask.rearrange("b (t p) -> (b t) p", p=P)
                         ).then_inc(mask_rows_loaded, 16)

            def loaded_once():
                sp.wait_ge(wqkv_loaded, 16 * KT)

            def load_rows(s):
                if not isinstance(s, int) or s > 0:
                    loaded_once()
                    job_done.wait(sp, s - 1, 0)
                    x_bias_written.wait(sp, s - 1, 1)
                rows = x[bass.ds(s, 1)].rearrange("b (t p) d -> p (b t) d", p=P)
                sp.dma_start(x_in[:, :, :], rows).then_inc(x_loaded.sem, 16)
                loaded_once()
                if not isinstance(s, int) or s > 0:
                    mask_read.wait(sp, s - 1, 1)
                else:
                    sp.wait_ge(setup_dve, MASK_ROWS_STEP)
                sp.dma_start(mask_in[:, :], nodemask[bass.ds(s, 1)].broadcast_to([P, N])
                             ).then_inc(mask_loaded.sem, 16)

            def load_adj(s, half, step, transposed):
                if transposed is not None:
                    loaded_once()
                    job_done.wait(sp, step, transposed + 1)
                cols = slice(half * N // 2, (half + 1) * N // 2)
                sp.dma_start(adj_in[:, :, :], adj[bass.ds(s, 1)].rearrange("b (t p) n -> p (b t) n", p=P)[:, :, cols]
                             ).then_inc(adj_loaded.sem, 16)

            def store_graph(s, g):
                loaded_once()
                out_written.wait(sp, s, 1)
                sp.dma_start(out[bass.ds(g, 1)].rearrange("b (t p) d -> p (b t) d", p=P), y[:, :, :]
                             ).then_inc(out_stored.sem, 16)

            def load_graph(s, plan):
                load_rows(s)
                load_adj(s - 1, 1, s - 1, plan.order["adj_transpose", 1])
                load_adj(s, 0, s - 1, plan.order["adj_transpose", NT - 1])

            sp.sem_inc(out_stored.sem, 16)
            load_rows(0)
            load_adj(0, 0, 0, None)
            load_graph(1, FIRST)
            with sp.Fori(2, B) as s:
                load_graph(s, FULL)
                store_graph(s - 1, s - 2)
            load_adj(B - 1, 1, B - 1, FINAL.order["adj_transpose", 1])
            store_graph(B - 1, B - 2)
            store_graph(B, B - 1)
            out_stored.wait(sp, B, 1, 16)

        @block.tensor
        def _(pe):
            def split_product(dst, pairs, ready=None):
                for n, (a_hi, a_lo, b_hi, b_lo) in enumerate(pairs):
                    if ready:
                        ready(n)
                    nc.tensor.matmul(dst, a_hi, b_hi, start=(n == 0), stop=False)
                    nc.tensor.matmul(dst, a_hi, b_lo, start=False, stop=False)
                    last = nc.tensor.matmul(dst, a_lo, b_hi, start=False, stop=(n == len(pairs) - 1))
                return last

            pe.wait_ge(ident_written, 1)
            pe.wait_ge(setup_dve, MASK_ROWS_STEP)
            nc.tensor.transpose(bank[0][:, 0:B * NT], mask_rows, ident[0:B * NT, 0:B * NT]).then_inc(setup_pe, 1)
            pe.wait_ge(setup_act, 2)
            for t in range(HT):
                for c in range(KT):
                    last = nc.tensor.transpose(
                        bank[1 + t // 2][:, (t % 2) * D + c * P:(t % 2) * D + (c + 1) * P],
                        wvh[:, c, t * P:(t + 1) * P], ident[:, :])
            last.then_inc(setup_pe, 1)
            pe.wait_ge(wv_loaded, 16)
            for t in range(KT):
                for c in range(KT):
                    last = nc.tensor.transpose(score_bank[0][:, t * D + c * P:t * D + (c + 1) * P],
                                               wv_raw[:, c, t * P:(t + 1) * P], ident[:, :])
            last.then_inc(setup_pe, 1)
            pe.wait_ge(setup_dve, PROJ_READY_STEP)
            for c in range(KT):
                for t in range(HT):
                    last = nc.tensor.matmul(score_bank[1][:, c * D:(c + 1) * D], wvh_t[:, t, c * P:(c + 1) * P],
                                            wout[:, t, :], start=(t == 0), stop=(t == HT - 1))
            last.then_inc(setup_pe, 1)
            for c in range(KT):
                for t in range(KT):
                    last = nc.tensor.matmul(turned_bank[0][:, 2 * c:2 * c + 2], wv1_t[:, t, c * P:(c + 1) * P],
                                            att_pairs[:, t, :], start=(t == 0), stop=(t == KT - 1))
            for t in range(KT):
                last = nc.tensor.matmul(turned_bank[1][:, 0:2], bv_rep[:, t, :], att_pairs[:, t, :],
                                        start=(t == 0), stop=(t == KT - 1))
            last.then_inc(setup_pe, 1)
            pe.wait_ge(setup_dve, SETUP_DVE_STEPS)

            def bank_read(plan, name, index):
                if name in SPLITS:
                    return split_written, 0, plan.split[name, index] + 1
                back = 1 if name in ("adj_product", "out_product") else 0
                return {"adj_transpose": edge_exp_written, "adj_product": adj_part_written,
                        "out_product": mix_written, "hop0": hop0_written, "source_score": edge_score_written,
                        "diffuse2": hop1_written, "diffuse1": hops_summed
                        }[name], back, NT if name == "source_score" else index + 1

            def begin(plan, s, name, index):
                n = plan.order[name, index] - RING
                if n >= 0:
                    signal, back, count = bank_read(plan, *plan.jobs[n][1:])
                    signal.wait(pe, s, count, back=back)
                elif plan.previous and -n <= len(plan.previous.jobs):
                    signal, back, count = bank_read(plan.previous, *plan.previous.jobs[n][1:])
                    if signal is split_written:
                        signal.wait(pe, s, count - len(plan.previous.split))
                    else:
                        signal.wait(pe, s, count, back=1 + back)
                return bank[plan.bank[name, index]]

            def split_ready(plan, s, name, index):
                split_written.wait(pe, s, plan.split[name, index] + 1)

            def tile(index):
                return slice(index * P, (index + 1) * P)

            def job(plan, s, name, index):
                done = job_done.sem
                b = begin(plan, s, name, index)
                if name in ("x_transpose", "x1_transpose", "adj_transpose"):
                    if name == "x_transpose" and index == 0:
                        x_loaded.wait(pe, s, 1, 16, back=-1)
                    elif name == "adj_transpose" and index % 2 == 0:
                        adj_loaded.wait(pe, s, index // 2 + 1, 16)
                    src = {"x_transpose": x_in, "x1_transpose": x1, "adj_transpose": adj_in}[name]
                    for t in range(NT):
                        if name == "x1_transpose" and index == 0:
                            x1_written.wait(pe, s, t + 1)
                        last = nc.tensor.transpose(b[:, tile(t)], src[:, t, tile(index % 2)], ident[:, :])
                elif name in ("query", "key"):
                    if index == 0:
                        split_ready(plan, s, "x_transpose", KT - 1)
                    kind = 0 if name == "query" else 1
                    last = split_product(b[:, :], [(wqkv_hi[:, t, kind, tile(index)], wqkv_lo[:, t, kind, tile(index)],
                                                    x_hi[:, t, :], x_lo[:, t, :]) for t in range(KT)])
                elif name == "value":
                    if index == 0:
                        split_written.wait(pe, s, 0)
                    last = split_product(b[:, :], [(x_hi[:, t, tile(index)], x_lo[:, t, tile(index)],
                                                    wqkv_hi[:, t, 2, :], wqkv_lo[:, t, 2, :]) for t in range(KT)])
                elif name == "mixed_value":
                    for half in range(2):
                        rows = tile(2 * index + half)
                        last = split_product(b[:, half * D:(half + 1) * D],
                                             [(x_hi[:, t, rows], x_lo[:, t, rows], wmix_hi[:, t, :], wmix_lo[:, t, :])
                                              for t in range(KT)])
                elif name == "adj_product":
                    def ready(j):
                        if index == 0:
                            if j == 0:
                                split_written.wait(pe, s, 0)
                            edge_split.wait(pe, s, j + 1)
                    last = split_product(b[:, 0:D], [(edge_hi[:, j, tile(index)], edge_lo[:, j, tile(index)],
                                                      mixed_hi[:, j, :], mixed_lo[:, j, :]) for j in range(NT)], ready)
                elif name == "out_product":
                    if index == 0:
                        split_ready(plan, s, "head_split", HT - 1)
                    for half in range(2):
                        last = split_product(b[:, half * D:(half + 1) * D],
                                             [head_rows(t, 2 * index + half)
                                              + (wout_hi[:, t, :], wout_lo[:, t, :]) for t in range(HT)])
                elif name == "hop0":
                    def ready(t):
                        if index == 0:
                            split_ready(plan, s, "x1_transpose", t)
                    last = split_product(b[:, 0:D + 2], [(x1_hi[:, t, tile(index)], x1_lo[:, t, tile(index)],
                                                          w0_hi[:, t, :], w0_lo[:, t, :]) for t in range(KT)], ready)
                elif name == "source_score":
                    last = split_product(b[:, :], [(wsrc_hi[:, t, :], wsrc_lo[:, t, :], x1_hi[:, t, :], x1_lo[:, t, :])
                                                   for t in range(KT)])
                elif name == "hop12":
                    last = split_product(b[:, :], [(x1_hi[:, t, tile(index)], x1_lo[:, t, tile(index)],
                                                    w12_hi[:, t, :], w12_lo[:, t, :]) for t in range(KT)])
                elif name == "diffuse2":
                    def ready(j):
                        if index == 0:
                            split_ready(plan, s, "hop12", j)
                            edge_split.wait(pe, s, NT + j + 1)
                    last = split_product(b[:, 0:D + 2], [(edge_hi[:, j, tile(index)], edge_lo[:, j, tile(index)],
                                                          hop_hi[:, j, :], hop_lo[:, j, :]) for j in range(NT)], ready)
                elif name == "diffuse1":
                    def ready(j):
                        if index == 0 and j % 2 == 0:
                            split_ready(plan, s, "hop1_split", j // 2)
                    last = split_product(b[:, 0:D], [(edge_hi[:, j, tile(index)], edge_lo[:, j, tile(index)],
                                                      hop_hi[:, j, 0:D], hop_lo[:, j, 0:D]) for j in range(NT)], ready)
                last.then_inc(done, 1)

            def score(s, plan, u):
                h, i = divmod(u, NT)
                pair, rows = h // 2, slice((h % 2) * DH, (h % 2 + 1) * DH)
                if u == 0:
                    split_written.wait(pe, s, 0)
                elif i == 0 and h % 2 == 0:
                    split_ready(plan, s, "key", pair)
                max_written.wait(pe, s, u - 1)
                split_product(score_bank[u % 2][:, :],
                              [(q_hi[rows, pair % 2, tile(i)], q_lo[rows, pair % 2, tile(i)],
                                k_hi[rows, pair % 2, :], k_lo[rows, pair % 2, :])]).then_inc(scores_done.sem, 1)

            def turn(s, back, u):
                probs_written.wait(pe, s, u + 1, back=back)
                turned_split.wait(pe, s, u - 1, back=back)
                for j in range(NT):
                    last = nc.tensor.transpose(turned_bank[u % 2][:, tile(j)], probs[:, u % BUFS, tile(j)], ident[:, :])
                last.then_inc(probs_turned.sem, 1)

            def weigh(s, plan, back, h, half):
                if h == 0 and half == 0:
                    split_ready(plan, s, "value", NT - 1)
                if half == 0:
                    head_written.wait(pe, s, h, back=back)
                if h == HEADS - 1 and half == 0:
                    value_kept.wait(pe, s, 1, back=back)
                turned_split.wait(pe, s, NT * h + 2 * half + 2, back=back)
                cols = slice(half * 2 * P, (half + 1) * 2 * P)
                for j in range(NT):
                    both = (last_value[:, j] if h == HEADS - 1 else value[:, j, h]).rearrange("p a d -> p (a d)")
                    nc.tensor.matmul(out_bank[:, cols], both, turned_hi[:, j, cols], start=(j == 0), stop=False)
                    last = nc.tensor.matmul(out_bank[:, cols], both, turned_lo[:, j, cols], start=False,
                                            stop=(j == NT - 1))
                last.then_inc(half_done.sem, 1)

            def step(s, plan):
                for slot in SLOTS:
                    if plan.layer0:
                        score(s, plan, slot)
                    for name, index in plan.slots[slot]:
                        job(plan, s, name, index)
                    if plan.unit(slot, 5) and slot % 2 == 1:
                        back, u = plan.unit(slot, 5)
                        weigh(s, plan, back, u // NT, u % NT // 2)
                    if plan.unit(slot, 2):
                        turn(s, *plan.unit(slot, 2))

            step(-1, BEFORE)
            step(0, FIRST)
            with pe.Fori(1, B - 1) as s:
                step(s, FULL)
            step(B - 1, FINAL)
            step(B, LAST)

        @block.scalar
        def _(act):
            for t in range(KT):
                act.wait_ge(wqkv_loaded, 16 * KT)
                cols = wqkv_raw[t].rearrange("p (h i d) -> p i h d", h=HEADS, i=3)
                nc.scalar.activation(wvh[:, t, :].rearrange("p (h d) -> p h d", h=HEADS), cols[:, 2], ACT.Copy
                                     ).then_inc(setup_act, 1)
            for t in range(KT):
                cols = wqkv_raw[t].rearrange("p (h i d) -> p i h d", h=HEADS, i=3)
                for i in range(3):
                    nc.scalar.activation(wqkv_hi[:, t, i, :].rearrange("p (h d) -> p h d", h=HEADS), cols[:, i],
                                         ACT.Copy).then_inc(setup_hi, 1)
            act.wait_ge(wk_loaded, 16 * KT)
            for t in range(KT):
                nc.scalar.activation(w12_hi[:, t, :].rearrange("p (k d) -> p k d", k=2), wk_raw[:, t, 1:3, :],
                                     ACT.Copy).then_inc(setup_hi, 1)
            for t in range(KT):
                act.wait_ge(setup_dve, ATT_PROJ_STEP)
                nc.scalar.activation(w0_hi[:, t, 0:D], wk_raw[:, t, 0, :], ACT.Copy).then_inc(setup_hi, 1)
                nc.scalar.activation(w0_hi[:, t, D:D + 2], att_proj[:, t, :], ACT.Copy).then_inc(setup_hi, 1)
                nc.scalar.activation(wsrc_hi[:, t, :], src_rep[:, t, :], ACT.Copy).then_inc(setup_hi, 1)
                nc.scalar.activation(wmix_hi[:, t, :], wmix_raw[:, t, :], ACT.Copy).then_inc(setup_hi, 1)
            for t in range(HT):
                nc.scalar.activation(wout_hi[:, t, :], wout[:, t, :], ACT.Copy).then_inc(setup_hi, 1)
            act.wait_ge(setup_dve, SETUP_DVE_STEPS)

            def split(plan, s, name, index):
                if name in plan_banks:
                    job_done.wait(act, s, plan.order[name, index] + 1)
                elif name == "hop1_split":
                    hop1_written.wait(act, s, 2 * index + 2)
                    job_done.wait(act, s, plan.order["diffuse2", NT - 1] + 1)
                elif name == "head_split":
                    head_written.wait(act, s, 2 * index + 2, back=0 if index < KT else 1)
                    if index >= KT:
                        job_done.wait(act, s, 0)
                    elif plan.layer1:
                        job_done.wait(act, s, plan.order["hop12", NT - 1] + 1)
                if name == "mixed_value":
                    b = bank[plan.bank[name, index]]
                    for half in range(2):
                        t = 2 * index + half
                        last = nc.scalar.activation(mixed_hi[:, t, :], b[:, half * D:(half + 1) * D], ACT.Identity,
                                                    scale=row_mask[:, t:t + 1])
                    last.then_inc(high_written.sem, 1)
                    return
                if name == "hop12":
                    nc.scalar.activation(hop1[:, index, :], bank[plan.bank[name, index]][:, 0:D], ACT.Copy)
                high, _ = parts(name, index)
                nc.scalar.activation(high, whole(plan, name, index), ACT.Copy).then_inc(high_written.sem, 1)

            plan_banks = {name for _, name, _ in FULL.jobs}

            def job(plan, s, name, index):
                if name in SPLITS:
                    split(plan, s, name, index)
                elif name == "adj_transpose":
                    b = bank[plan.bank[name, index]]
                    job_done.wait(act, s, plan.order[name, index] + 1)
                    nc.scalar.activation(adj_t[:, index, :], b[:, :], ACT.Copy)
                    if plan.layer1:
                        edge_split.wait(act, s, NT + index + 1)
                    nc.scalar.activation(edge[:, index, :], b[:, :], ACT.Exp, scale=-1.0
                                         ).then_inc(edge_exp_written.sem, 1)
                elif name == "edge_score":
                    job_done.wait(act, s, plan.order["source_score", 0] + 1)
                    hop0_written.wait(act, s, NT)
                    if index == 0:
                        edge_split.wait(act, s, NT)
                    nc.scalar.activation(edge[:, index, :], bank[plan.bank["source_score", 0]][:, :], ACT.Identity,
                                         bias=target_score[:, index:index + 1]).then_inc(edge_score_written.sem, 1)
                elif name == "alpha_exp":
                    leaky_written.wait(act, s, index + 1)
                    nc.scalar.activation(edge[:, index, :], edge[:, index, :], ACT.Exp
                                         ).then_inc(alpha_exp_written.sem, 1)

                elif name in ("edge_split", "alpha_split"):
                    if name == "alpha_split":
                        alpha_written.wait(act, s, index + 1)
                    else:
                        edge_written.wait(act, s, index + 1, back=1)
                        job_done.wait(act, s, 0)
                    nc.scalar.activation(edge_hi[:, index, :], edge[:, index, :], ACT.Copy).then_inc(edge_high.sem, 1)
                elif name == "normalize0":
                    shift0_written.wait(act, s, 1)
                    for t in range(NT):
                        nc.scalar.activation(x1[:, t, :], mix[:, t, :], ACT.Identity, bias=shift0[:, t:t + 1],
                                             scale=rstd0[:, t:t + 1]).then_inc(x1_written.sem, 1)
                elif name == "normalize1":
                    shift1_written.wait(act, s, 1)
                    for t in range(NT):
                        last = nc.scalar.activation(y[:, t, :], y[:, t, :], ACT.Identity, bias=shift1[:, t:t + 1],
                                                    scale=rstd1[:, t:t + 1])
                    last.then_inc(out_written.sem, 1)
                elif name == "keep_value":
                    split_written.wait(act, s, plan.split["value", NT - 1] + 1)
                    nc.scalar.activation(last_value[:, :, :, :], f32(value[:, :, HEADS - 1, :, :]), ACT.Copy
                                         ).then_inc(value_kept.sem, 1)

            def exponent(s, back, u):
                i, half = u % NT, probs[:, u % BUFS, :]
                exp_bias_written.wait(act, s, u + 1, back=back)
                nc.scalar.activation(half, half, ACT.Exp, bias=exp_bias[:, u % 2:u % 2 + 1],
                                     scale=row_scale[:, i:i + 1], accum_out=row_sum[:, i:i + 1]
                                     ).then_inc(exp_written.sem, 1)

            def turned(ap_of, u):
                return ap_of[:, :, (u % NT) * P:(u % NT + 1) * P]

            def split_turned(s, back, u):
                probs_turned.wait(act, s, u + 1, back=back)
                half_done.wait(act, s, u // 2 - 1, back=back)
                nc.scalar.activation(turned(turned_hi, u), turned_bank[u % 2][:, :].rearrange("p (j i) -> p j i", j=NT),
                                     ACT.Copy).then_inc(turned_high.sem, 1)

            def take_head(s, plan, back, h):
                rows = slice((h % 2) * DH, (h % 2 + 1) * DH)
                half_done.wait(act, s, 2 * h + 2, back=back)
                if h % NT == 0 or h % NT == 2:
                    index = (h // 2 + 2) % HT
                    if back:
                        split_written.wait(act, s, 0)
                    elif plan.layer1 or h >= NT:
                        split_written.wait(act, s, plan.split["head_split", index] + 1)
                nc.scalar.activation(heads[rows, h // 2 % 2, :], out_bank[DH:2 * DH, :], ACT.Copy
                                     ).then_inc(head_low_copied.sem, 1)

            def step(s, plan):
                for slot in SLOTS:
                    if plan.unit(slot, 1):
                        exponent(s, *plan.unit(slot, 1))
                    for name, index in plan.taken[slot]:
                        job(plan, s, name, index)
                    if plan.unit(slot, 3):
                        split_turned(s, *plan.unit(slot, 3))
                    if plan.unit(slot, 8) and slot % NT == 0:
                        back, u = plan.unit(slot, 8)
                        take_head(s, plan, back, u // NT)
                    for name, index in plan.side[slot]:
                        job(plan, s, name, index)

            step(-1, BEFORE)
            step(0, FIRST)
            with act.Fori(1, B - 1) as s:
                step(s, FULL)
            step(B - 1, FINAL)
            step(B, LAST)

        @block.vector
        def _(dve):
            setup = [0]

            def link(instruction):
                setup[0] += 1
                instruction.then_inc(setup_dve, 1)
                dve.wait_ge(setup_dve, setup[0])

            dve.wait_ge(mask_rows_loaded, 16)
            link(nc.vector.tensor_copy(mask_rows, mask_rows_u8))
            assert setup[0] == MASK_ROWS_STEP
            dve.wait_ge(small_loaded, 16 * 5)
            for t in range(KT):
                for o in range(2):
                    link(nc.vector.tensor_copy(att_pairs[:, t, o:o + 1], att_cols[:, o * KT + t, :]))
            dve.wait_ge(const_written, 1)
            for t in range(KT):
                link(nc.vector.tensor_scalar(bv_rep[:, t, :], ones, bv_cols[:, t, :], None, ALU.mult))
            dve.wait_ge(wout_loaded, 16)
            link(nc.vector.tensor_scalar(wout[:, :, :], wout[:, :, :], GAIN, None, ALU.mult))
            dve.wait_ge(setup_pe, 1)
            link(nc.vector.tensor_copy(mask_col[:, :], bank[0][:, 0:B * NT]))
            dve.wait_ge(setup_pe, 2)
            for t in range(HT):
                link(nc.vector.tensor_copy(wvh_t[:, t, :], bank[1 + t // 2][:, (t % 2) * D:(t % 2 + 1) * D]))
            dve.wait_ge(setup_pe, 3)
            link(nc.vector.tensor_copy(wv1_t, score_bank[0][:, :].rearrange("p (t d) -> p t d", t=KT)))
            assert setup[0] == PROJ_READY_STEP
            dve.wait_ge(setup_pe, 4)
            link(nc.vector.tensor_copy(wmix_raw, score_bank[1][:, :].rearrange("p (t d) -> p t d", t=KT)))
            dve.wait_ge(setup_pe, 5)
            link(nc.vector.tensor_copy(att_proj, turned_bank[0][:, 0:2 * KT].rearrange("p (t o) -> p t o", t=KT)))
            link(nc.vector.tensor_copy(bv_proj, turned_bank[1][:, 0:2]))
            link(nc.vector.tensor_tensor(score_const[:, :], bv_proj[:, 0:1], bv_proj[:, 1:2], ALU.add))
            link(nc.vector.tensor_tensor(score_const[:, :], score_const[:, :], att_b_all, ALU.add))
            for t in range(KT):
                link(nc.vector.tensor_scalar(src_rep[:, t, :], ones, att_proj[:, t, 1:2], None, ALU.mult))
            assert setup[0] == ATT_PROJ_STEP
            hi = 0
            for t in range(KT):
                cols = wqkv_raw[t].rearrange("p (h i d) -> p i h d", h=HEADS, i=3)
                for i in range(3):
                    hi += 1
                    dve.wait_ge(setup_hi, hi)
                    link(nc.vector.tensor_tensor(
                        wqkv_lo[:, t, i, :].rearrange("p (h d) -> p h d", h=HEADS), cols[:, i],
                        f32(wqkv_hi[:, t, i, :]).rearrange("p (h d) -> p h d", h=HEADS), ALU.subtract))
            for t in range(KT):
                hi += 1
                dve.wait_ge(setup_hi, hi)
                link(nc.vector.tensor_tensor(w12_lo[:, t, :].rearrange("p (k d) -> p k d", k=2), wk_raw[:, t, 1:3, :],
                                             f32(w12_hi[:, t, :]).rearrange("p (k d) -> p k d", k=2), ALU.subtract))
            for t in range(KT):
                for lo, raw, high in ((w0_lo[:, t, 0:D], wk_raw[:, t, 0, :], w0_hi[:, t, 0:D]),
                                      (w0_lo[:, t, D:D + 2], att_proj[:, t, :], w0_hi[:, t, D:D + 2]),
                                      (wsrc_lo[:, t, :], src_rep[:, t, :], wsrc_hi[:, t, :]),
                                      (wmix_lo[:, t, :], wmix_raw[:, t, :], wmix_hi[:, t, :])):
                    hi += 1
                    dve.wait_ge(setup_hi, hi)
                    link(nc.vector.tensor_tensor(lo, raw, f32(high), ALU.subtract))
            for t in range(HT):
                hi += 1
                dve.wait_ge(setup_hi, hi)
                link(nc.vector.tensor_tensor(wout_lo[:, t, :], wout[:, t, :], f32(wout_hi[:, t, :]), ALU.subtract))
            link(nc.vector.tensor_tensor(bk_sum[:, :], bk_raw[:, 0, :], bk_raw[:, 1, :], ALU.add))
            link(nc.vector.tensor_tensor(bk_sum[:, :], bk_sum[:, :], bk_raw[:, 2, :], ALU.add))
            link(nc.vector.tensor_copy(hop_hi[:, :, D:D + 2], ones_pairs))
            link(nc.vector.tensor_scalar(hop_lo[:, :, D:D + 2], ones_pairs, 0.0, None, ALU.mult))
            link(nc.vector.memset(neg_half[:, :], -0.5))
            assert setup[0] == SETUP_DVE_STEPS, setup[0]

            def mask_columns(s):
                mask_loaded.wait(dve, s, 1, 16)
                nc.vector.tensor_scalar(column_bias[:, :], mask_in[:, :], -1.0, MASKED, ALU.add, ALU.mult
                                        ).then_inc(mask_read.sem, 1)
                mask_read.wait(dve, s, 1)

            def mask_rows_of(s):
                exp_written.wait(dve, s, 0)
                col = mask_col[:, bass.ds(s * NT, NT)]
                nc.vector.tensor_copy(row_mask[:, :], col)
                nc.vector.tensor_scalar(row_scale[:, :], col, SCORE_SCALE, None, ALU.mult)
                nc.vector.tensor_scalar(row_neg_scale[:, :], col, -SCORE_SCALE, None, ALU.mult
                                        ).then_inc(row_masks_written.sem, 1)
                row_masks_written.wait(dve, s, 1)

            def score_max(s, u):
                scores_done.wait(dve, s, u + 1)
                probs_turned.wait(dve, s, u - BUFS + 1)
                nc.vector.memset(wait_carrier[:, :], 0.0)
                nc.vector.tensor_tensor_reduce(
                    out=probs[:, u % BUFS, :], in0=score_bank[u % 2][:, :], in1=column_bias[:, :], scale=1.0,
                    scalar=LOWEST, op0=ALU.add, op1=ALU.max, accum_out=row_max[:, u % 2:u % 2 + 1]
                ).then_inc(max_written.sem, 1)

            def bias(s, u):
                i = u % NT
                max_written.wait(dve, s, u + 1)
                nc.vector.tensor_tensor(exp_bias[:, u % 2:u % 2 + 1], row_max[:, u % 2:u % 2 + 1],
                                        row_neg_scale[:, i:i + 1], ALU.mult).then_inc(exp_bias_written.sem, 1)

            def invert_sum(s, back, u):
                i = u % NT
                exp_written.wait(dve, s, u + 1, back=back)
                nc.vector.reciprocal(row_inv[:, i:i + 1], row_sum[:, i:i + 1]).then_inc(inv_written.sem, 1)

            def split_turned(s, back, u):
                cols = slice((u % NT) * P, (u % NT + 1) * P)
                turned_high.wait(dve, s, u + 1, back=back)
                nc.vector.tensor_tensor(
                    turned_lo[:, :, cols], turned_bank[u % 2][:, :].rearrange("p (j i) -> p j i", j=NT),
                    f32(turned_hi[:, :, cols]), ALU.subtract).then_inc(turned_split.sem, 1)

            def take_head(s, plan, back, h):
                rows = slice((h % 2) * DH, (h % 2 + 1) * DH)
                head_low_copied.wait(dve, s, h + 1, back=back)
                nc.vector.tensor_tensor(heads[rows, h // 2 % 2, :], out_bank[0:DH, :], heads[rows, h // 2 % 2, :], ALU.add
                                        ).then_inc(head_written.sem, 1)

            def moments(s, stats, mean, var, neg_mean, signal):
                signal.wait(dve, s, NT)
                nc.vector.memset(wait_carrier[:, :], 0.0)
                for t in range(NT):
                    nc.vector.bn_aggr(mean[:, t, :], stats[:, t, :]).then_inc(signal.sem, 1)
                signal.wait(dve, s, 2 * NT)
                nc.vector.tensor_scalar(neg_mean[:, :], mean[:, :, 0], -1.0, None, ALU.mult)
                nc.vector.tensor_scalar(var[:, :], mean[:, :, 1], EPS_NORM, None, ALU.add).then_inc(signal.sem, 1)

            def split(plan, s, name, index):
                high_written.wait(dve, s, plan.split[name, index] + 1)
                if name == "mixed_value":
                    b = bank[plan.bank[name, index]]
                    for half in range(2):
                        t = 2 * index + half
                        last = nc.vector.scalar_tensor_tensor(
                            out=mixed_lo[:, t, :], in0=b[:, half * D:(half + 1) * D], scalar=row_mask[:, t:t + 1],
                            in1=f32(mixed_hi[:, t, :]), op0=ALU.mult, op1=ALU.subtract)
                    last.then_inc(split_written.sem, 1)
                    return
                high, low = parts(name, index)
                nc.vector.tensor_tensor(low, whole(plan, name, index), f32(high), ALU.subtract
                                        ).then_inc(split_written.sem, 1)

            def job(plan, s, name, index):
                if name in SPLITS:
                    split(plan, s, name, index)
                elif name == "keep_mask":
                    nc.vector.tensor_copy(closing_mask[:, :], row_mask[:, :]).then_inc(mask_kept.sem, 1)
                elif name == "stats0":
                    mix_written.wait(dve, s, index + 1, back=1)
                    for t in (2 * index, 2 * index + 1):
                        nc.vector.bn_stats(stats0[:, t, :], mix[:, t, :]).then_inc(moments0.sem, 1)
                elif name == "moments0":
                    moments(s, stats0, mean0, var0, neg_mean0, moments0)
                elif name == "moments1":
                    moments(s, stats1, mean1, var1, neg_mean1, moments1)
                elif name == "leaky":
                    scores = edge[:, index, :]
                    edge_score_written.wait(dve, s, index + 1)
                    nc.vector.scalar_tensor_tensor(out=scores, in0=scores, scalar=SLOPE, in1=scores,
                                                   op0=ALU.mult, op1=ALU.max).then_inc(leaky_written.sem, 1)
                elif name == "adj_product":
                    job_done.wait(dve, s, plan.order[name, index] + 1)
                    if index == 0:
                        x_bias_written.wait(dve, s, 1, back=1)
                        mask_kept.wait(dve, s, 1, back=1)
                    nc.vector.scalar_tensor_tensor(
                        out=mix[:, index, :], in0=bank[plan.bank[name, index]][:, 0:D],
                        scalar=closing_mask[:, index:index + 1], in1=mix[:, index, :], op0=ALU.mult, op1=ALU.add
                    ).then_inc(adj_part_written.sem, 1)
                elif name == "out_product":
                    rows = slice(2 * index, 2 * index + 2)
                    job_done.wait(dve, s, plan.order[name, index] + 1)
                    adj_part_written.wait(dve, s, 2 * index + 2, back=1)
                    nc.vector.tensor_tensor(mix[:, rows, :], halves(bank[plan.bank[name, index]]), mix[:, rows, :],
                                            ALU.add).then_inc(mix_written.sem, 1)
                elif name == "hop0":
                    b = bank[plan.bank[name, index]]
                    if index == 0:
                        out_stored.wait(dve, s, 0, 16)
                    job_done.wait(dve, s, plan.order[name, index] + 1)
                    nc.vector.tensor_tensor(y[:, index, :], b[:, 0:D], bk_sum[:, :], ALU.add)
                    nc.vector.tensor_tensor(target_score[:, index:index + 1], b[:, D:D + 1], score_const[:, :],
                                            ALU.add).then_inc(hop0_written.sem, 1)
                elif name == "diffuse2":
                    b = bank[plan.bank[name, index]]
                    job_done.wait(dve, s, plan.order[name, index] + 1)
                    nc.vector.tensor_scalar(alpha_sum[:, index:index + 1], b[:, D:D + 1], EPS_SUM, None, ALU.add
                                            ).then_inc(alpha_sum_written.sem, 1)
                    alpha_sum_written.wait(dve, s, index + 1)
                    nc.vector.reciprocal(alpha_inv[:, index:index + 1], alpha_sum[:, index:index + 1]
                                         ).then_inc(alpha_inv_written.sem, 1)
                    alpha_inv_written.wait(dve, s, index + 1)
                    nc.vector.scalar_tensor_tensor(
                        out=hop1[:, index, :], in0=b[:, 0:D], scalar=alpha_inv[:, index:index + 1],
                        in1=hop1[:, index, :], op0=ALU.mult, op1=ALU.add).then_inc(hop1_written.sem, 1)
                elif name == "diffuse1":
                    job_done.wait(dve, s, plan.order[name, index] + 1)
                    nc.vector.scalar_tensor_tensor(
                        out=y[:, index, :], in0=bank[plan.bank[name, index]][:, 0:D],
                        scalar=alpha_inv[:, index:index + 1], in1=y[:, index, :], op0=ALU.mult, op1=ALU.add
                    ).then_inc(hops_summed.sem, 1)
                    hops_summed.wait(dve, s, index + 1)
                    nc.vector.scalar_tensor_tensor(out=y[:, index, :], in0=y[:, index, :], scalar=0.0,
                                                   in1=x1[:, index, :], op0=ALU.max, op1=ALU.add
                                                   ).then_inc(y_written.sem, 1)
                    y_written.wait(dve, s, index + 1)
                    nc.vector.bn_stats(stats1[:, index, :], y[:, index, :]).then_inc(moments1.sem, 1)

            def step(s, plan):
                for slot in SLOTS:
                    if plan.layer0:
                        if slot == 0:
                            mask_columns(s)
                        score_max(s, slot)
                    if plan.unit(slot, 1):
                        invert_sum(s, *plan.unit(slot, 1))
                    if plan.layer0:
                        if slot == 0:
                            mask_rows_of(s)
                        bias(s, slot)
                    for name, index in plan.taken[slot]:
                        job(plan, s, name, index)
                    if plan.unit(slot, 3):
                        split_turned(s, *plan.unit(slot, 3))
                    if plan.unit(slot, 8) and slot % NT == 0:
                        back, u = plan.unit(slot, 8)
                        take_head(s, plan, back, u // NT)
                    for name, index in plan.side[slot]:
                        job(plan, s, name, index)

            step(-1, BEFORE)
            step(0, FIRST)
            with dve.Fori(1, B - 1) as s:
                step(s, FULL)
            step(B - 1, FINAL)
            step(B, LAST)

        @block.gpsimd
        def _(pool):
            nc.gpsimd.memset(ones, 1.0).then_inc(const_written, 1)
            pool.wait_ge(const_written, 1)
            nc.gpsimd.affine_select(out=ident[:, :], in_=ones, compare_op=ALU.is_equal, fill=0.0, base=0,
                                    pattern=[[-1, P]], channel_multiplier=1).then_inc(ident_written, 1)
            pool.wait_ge(small_loaded, 16 * 5)
            pool.wait_ge(setup_dve, SETUP_DVE_STEPS)

            def reciprocal_root(s, moments, rstd, var, neg_mean, shift, written, shift_written):
                moments.wait(pool, s, 2 * NT + 1)
                nc.gpsimd.tensor_tensor(rstd[:, :], var[:, :], neg_half[:, :], ALU.pow).then_inc(written.sem, 1)
                written.wait(pool, s, 1)
                nc.gpsimd.tensor_tensor(shift[:, :], neg_mean[:, :], rstd[:, :], ALU.mult
                                        ).then_inc(shift_written.sem, 1)

            def normalize(s, back, u):
                i = u % NT
                inv_written.wait(pool, s, u + 1, back=back)
                nc.gpsimd.tensor_tensor(probs[:, u % BUFS, :], probs[:, u % BUFS, :],
                                        row_inv[:, i:i + 1].broadcast_to([P, N]), ALU.mult
                                        ).then_inc(probs_written.sem, 1)

            def add_bias(s, plan, t):
                if t == 0:
                    x_loaded.wait(pool, s, 1, 16)
                    if plan.layer1:
                        x1_written.wait(pool, s, NT)
                last = nc.gpsimd.tensor_tensor(mix[:, t, :], x_in[:, t, :], b_out_all[:, :], ALU.add)
                if t == NT - 1:
                    last.then_inc(x_bias_written.sem, 1)

            def step(s, plan):
                for slot in SLOTS:
                    if plan.unit(slot, 1):
                        normalize(s, *plan.unit(slot, 1))
                    if plan.layer0 and X_BIAS_SLOT <= slot < X_BIAS_SLOT + NT:
                        add_bias(s, plan, slot - X_BIAS_SLOT)
                    for name, index in plan.taken[slot] + plan.side[slot]:
                        weights = edge[:, index, :]
                        if name == "moments0":
                            reciprocal_root(s, moments0, rstd0, var0, neg_mean0, shift0, rstd0_written, shift0_written)
                        elif name == "moments1":
                            reciprocal_root(s, moments1, rstd1, var1, neg_mean1, shift1, rstd1_written, shift1_written)
                        elif name in ("edge_split", "alpha_split"):
                            edge_high.wait(pool, s, (0 if name == "edge_split" else NT) + index + 1)
                            nc.gpsimd.tensor_tensor(edge_lo[:, index, :], weights, f32(edge_hi[:, index, :]), ALU.subtract
                                                    ).then_inc(edge_split.sem, 1)
                        elif name == "alpha_exp":
                            alpha_exp_written.wait(pool, s, index + 1)
                            nc.gpsimd.tensor_tensor(weights, weights, adj_t[:, index, :], ALU.mult
                                                    ).then_inc(alpha_written.sem, 1)
                        elif name == "adj_transpose":
                            edge_exp_written.wait(pool, s, index + 1)
                            nc.gpsimd.tensor_tensor(weights, weights, adj_t[:, index, :], ALU.add
                                                    ).then_inc(edge_written.sem, 1)

            step(-1, BEFORE)
            step(0, FIRST)
            with pool.Fori(1, B - 1) as s:
                step(s, FULL)
            step(B - 1, FINAL)
            step(B, LAST)


MASK_ROWS_STEP = 1
PROJ_READY_STEP = MASK_ROWS_STEP + 4 + 2 + 1 + 1 + 4 + 1
ATT_PROJ_STEP = PROJ_READY_STEP + 1 + 2 + 2 + 2
SETUP_DVE_STEPS = ATT_PROJ_STEP + 6 + 2 + 8 + 4 + 2 + 3

_INS = ['x', 'adj', 'nodemask', 'L0_gnn_W_qkv', 'L0_gnn_W_out', 'L0_gnn_b_out', 'L1_gnn_Wv', 'L1_gnn_bv',
        'L1_gnn_aw', 'L1_gnn_ab', 'L1_gnn_Wk', 'L1_gnn_bk']


def kernel(**inputs):
    import numpy as _np
    import concourse.bacc as _bacc
    from concourse import mybir as _mybir
    from concourse.bass_utils import run_bass_kernel_spmd as _run

    nc = _bacc.Bacc("TRN2", target_bir_lowering=False, num_devices=1)
    arrays, args = {}, []
    for name in _INS:
        a = _np.ascontiguousarray(inputs[name])
        arrays[f"in_{name}_dram"] = a
        args.append(nc.dram_tensor(f"in_{name}_dram", a.shape, _mybir.dt.from_np(a.dtype), kind="ExternalInput").ap())
    shape = inputs["x"].shape
    args.append(nc.dram_tensor("out_0_dram", shape, _mybir.dt.float32, kind="ExternalOutput").ap())
    graph_layers(nc, *args)
    r = _run(nc, [arrays], core_ids=[0])
    return r.results[0]["out_0_dram"]
```
